# Optimizing a Trainium2 kernel written in Bass

```python
import numpy as np
import jax
import jax.numpy as jnp

def _softmax(x, axis=-1):
    return jax.nn.softmax(x, axis=axis)

def _gelu(x):
    return jax.nn.gelu(x, approximate=True)

def _silu(x):
    return jax.nn.silu(x)

def _sigmoid(x):
    return jax.nn.sigmoid(x)

def _layernorm(x, axis=-1, eps=1e-05):
    m = jnp.mean(x, axis=axis, keepdims=True)
    v = jnp.var(x, axis=axis, keepdims=True)
    return (x - m) / jnp.sqrt(v + eps)

def _scatter_add(tgt, idx, src, axis=0):
    return tgt.at[idx].add(src)

def _segment_sum(src, seg, n):
    return jax.ops.segment_sum(src, seg, n)
kernel_name = 'mk_cond_resid_d4_seqx_r2_cf53df'

def setup_inputs(seed: int=0):
    np.random.seed(seed)
    _w = jnp.asarray

    def _rec_inputs():
        import jax
        import jax.numpy as jnp
        _rk = jax.random.key(seed)
        x = -1.528e-05 + 0.9999 * jax.random.normal(jax.random.fold_in(_rk, 1), (2, 2048, 512), jnp.float32)
        _lenS = 2048 - jax.random.randint(jax.random.fold_in(_rk, 7), (2,), 0, max(1, 2048 // 4) + 1, jnp.int32)
        _lenS2 = 2048 - jax.random.randint(jax.random.fold_in(_rk, 8), (2,), 0, max(1, 2048 // 4) + 1, jnp.int32)
        cond_1024 = -0.00608245 + 1.00131 * jax.random.normal(jax.random.fold_in(_rk, 11), (2, 512), jnp.float32)
        itok_BxS_2_50255 = jax.random.randint(jax.random.fold_in(_rk, 12), (2, 2048), 2, 25128, jnp.int32)
        return (x, cond_1024, itok_BxS_2_50255)
    x, cond_1024, itok_BxS_2_50255 = _rec_inputs()

    def _L0_cond_setup():
        import jax, jax.numpy as jnp
        import numpy as np
        LATENT = 512
        key = jax.random.key(seed)
        k1, k2, k3, k4 = jax.random.split(key, 4)
        B, T, D = (64, 256, LATENT)
        h_t = jax.random.normal(k1, (B, D), dtype=jnp.float32)
        z = jax.random.normal(k2, (B, T, D), dtype=jnp.float32)
        bound = 1.0 / np.sqrt(2 * D)
        W = jax.random.uniform(k3, (D, 2 * D), minval=-bound, maxval=bound, dtype=jnp.float32)
        b = jax.random.uniform(k4, (D,), minval=-bound, maxval=bound, dtype=jnp.float32)
        alpha = jnp.full((D,), 0.1, dtype=jnp.float32)
        return {'h_t': h_t, 'z': z, 'W': W, 'b': b, 'alpha': alpha}
    _L0_cond_all = _L0_cond_setup()
    _L0_cond_in = {k: v for k, v in _L0_cond_all.items() if k in ('W', 'b', 'alpha')}
    del _L0_cond_all

    def _L1_cond_setup():
        import jax, jax.numpy as jnp
        import numpy as np
        HASH_PRIME = 5099
        MIN_CAPACITY = 4
        key = jax.random.key(seed)
        ks = jax.random.split(key, 8)
        B, T, D, F, E = (8, 1024, 512, 1024, 16)
        return {'x': jax.random.normal(ks[0], (B, T, D), dtype=jnp.float32), 'token_ids': jax.random.randint(ks[1], (B, T), 0, 50257, dtype=jnp.int32), 'shift_state': jax.random.normal(ks[2], (B, D), dtype=jnp.float32), 'time_maa_k': jax.random.uniform(ks[3], (D,), dtype=jnp.float32), 'time_maa_r': jax.random.uniform(ks[4], (D,), dtype=jnp.float32), 'w_recept': jax.random.normal(ks[5], (D, D), dtype=jnp.float32) * 0.02, 'w_key': jax.random.normal(ks[6], (E, D, F), dtype=jnp.float32) * 0.02, 'w_value': jax.random.normal(ks[7], (E, F, D), dtype=jnp.float32) * 0.02}
    _L1_cond_all = _L1_cond_setup()
    _L1_cond_in = {k: v for k, v in _L1_cond_all.items() if k in ('time_maa_k', 'time_maa_r', 'w_recept', 'w_key', 'w_value')}
    del _L1_cond_all

    def _L2_cond_setup():
        import jax, jax.numpy as jnp
        import numpy as np
        B, T, D_IN, V_IN, E = (64, 128, 512, 512, 512)
        key = jax.random.key(seed)
        ks = jax.random.split(key, 16)
        s = 0.01
        return {'video': jax.random.normal(ks[0], (B, V_IN), jnp.float32), 'seq': jax.random.normal(ks[1], (B, T, D_IN), jnp.float32), 'W_z': jax.random.normal(ks[2], (D_IN, E), jnp.float32) * s, 'U_z': jax.random.normal(ks[3], (E, E), jnp.float32) * s, 'C_z': jax.random.normal(ks[4], (V_IN, E), jnp.float32) * s, 'b_z': jnp.zeros((E,), jnp.float32), 'W_r': jax.random.normal(ks[5], (D_IN, E), jnp.float32) * s, 'U_r': jax.random.normal(ks[6], (E, E), jnp.float32) * s, 'C_r': jax.random.normal(ks[7], (V_IN, E), jnp.float32) * s, 'b_r': jnp.zeros((E,), jnp.float32), 'W': jax.random.normal(ks[8], (D_IN, E), jnp.float32) * s, 'U': jax.random.normal(ks[9], (E, E), jnp.float32) * s, 'C': jax.random.normal(ks[10], (V_IN, E), jnp.float32) * s, 'b': jnp.zeros((E,), jnp.float32)}
    _L2_cond_all = _L2_cond_setup()
    _L2_cond_in = {k: v for k, v in _L2_cond_all.items() if k in ('W_z', 'U_z', 'C_z', 'b_z', 'W_r', 'U_r', 'C_r', 'b_r', 'W', 'U', 'C', 'b')}
    del _L2_cond_all

    def _L3_cond_setup():
        import jax, jax.numpy as jnp
        import numpy as np
        B, T, D = (128, 32, 512)
        ADA, INTER, RANK = (512, 512, 8)
        LN_EPS = 1e-05

        def _layernorm(x, g, b):
            mu = jnp.mean(x, axis=-1, keepdims=True)
            var = jnp.var(x, axis=-1, keepdims=True)
            return (x - mu) * jax.lax.rsqrt(var + LN_EPS) * g + b
        key = jax.random.key(seed)
        ks = jax.random.split(key, 9)
        return {'x': jax.random.normal(ks[0], (B, T, D), dtype=jnp.float32), 'ada_emb': jax.random.normal(ks[1], (B, ADA), dtype=jnp.float32), 'base_layer': jax.random.normal(ks[2], (D, D), dtype=jnp.float32), 'w1': jax.random.normal(ks[3], (ADA, INTER), dtype=jnp.float32) * 0.02, 'b1': jnp.zeros((INTER,), dtype=jnp.float32), 'w2': jax.random.normal(ks[4], (INTER, 2 * D * RANK), dtype=jnp.float32) * 0.02, 'b2': jnp.zeros((2 * D * RANK,), dtype=jnp.float32), 'ln_g': jnp.ones((ADA,), dtype=jnp.float32), 'ln_b': jnp.zeros((ADA,), dtype=jnp.float32)}
    _L3_cond_all = _L3_cond_setup()
    _L3_cond_in = {k: v for k, v in _L3_cond_all.items() if k in ('base_layer', 'w1', 'b1', 'w2', 'b2', 'ln_g', 'ln_b')}
    del _L3_cond_all
    return {'x': x, 'cond_1024': cond_1024, 'itok_BxS_2_50255': itok_BxS_2_50255, 'L0_cond_W': _L0_cond_in['W'], 'L0_cond_b': _L0_cond_in['b'], 'L0_cond_alpha': _L0_cond_in['alpha'], 'L1_cond_time_maa_k': _L1_cond_in['time_maa_k'], 'L1_cond_time_maa_r': _L1_cond_in['time_maa_r'], 'L1_cond_w_recept': _L1_cond_in['w_recept'], 'L1_cond_w_key': _L1_cond_in['w_key'], 'L1_cond_w_value': _L1_cond_in['w_value'], 'L2_cond_W_z': _L2_cond_in['W_z'], 'L2_cond_U_z': _L2_cond_in['U_z'], 'L2_cond_C_z': _L2_cond_in['C_z'], 'L2_cond_b_z': _L2_cond_in['b_z'], 'L2_cond_W_r': _L2_cond_in['W_r'], 'L2_cond_U_r': _L2_cond_in['U_r'], 'L2_cond_C_r': _L2_cond_in['C_r'], 'L2_cond_b_r': _L2_cond_in['b_r'], 'L2_cond_W': _L2_cond_in['W'], 'L2_cond_U': _L2_cond_in['U'], 'L2_cond_C': _L2_cond_in['C'], 'L2_cond_b': _L2_cond_in['b'], 'L3_cond_base_layer': _L3_cond_in['base_layer'], 'L3_cond_w1': _L3_cond_in['w1'], 'L3_cond_b1': _L3_cond_in['b1'], 'L3_cond_w2': _L3_cond_in['w2'], 'L3_cond_b2': _L3_cond_in['b2'], 'L3_cond_ln_g': _L3_cond_in['ln_g'], 'L3_cond_ln_b': _L3_cond_in['ln_b']}

def reference(x, cond_1024, itok_BxS_2_50255, L0_cond_W, L0_cond_b, L0_cond_alpha, L1_cond_time_maa_k, L1_cond_time_maa_r, L1_cond_w_recept, L1_cond_w_key, L1_cond_w_value, L2_cond_W_z, L2_cond_U_z, L2_cond_C_z, L2_cond_b_z, L2_cond_W_r, L2_cond_U_r, L2_cond_C_r, L2_cond_b_r, L2_cond_W, L2_cond_U, L2_cond_C, L2_cond_b, L3_cond_base_layer, L3_cond_w1, L3_cond_b1, L3_cond_w2, L3_cond_b2, L3_cond_ln_g, L3_cond_ln_b):
    import jax
    import jax.numpy as jnp

    def _L0_cond_ref(h_t, z, W, b, alpha):
        import jax, jax.numpy as jnp
        import numpy as np
        LATENT = 512
        D = h_t.shape[-1]
        Wh = W[:, :D]
        Wz = W[:, D:]
        leak = 1.0 - alpha

        def step(h, z_t):
            gate = jax.nn.sigmoid(h @ Wh.T + z_t @ Wz.T + b)
            h_new = jnp.tanh(h * leak + gate * z_t)
            return (h_new, h_new)
        _, hs = jax.lax.scan(step, h_t, jnp.swapaxes(z, 0, 1))
        return jnp.swapaxes(hs, 0, 1)

    def _L1_cond_ref(x, token_ids, shift_state, time_maa_k, time_maa_r, w_recept, w_key, w_value):
        import jax, jax.numpy as jnp
        import numpy as np
        HASH_PRIME = 5099
        MIN_CAPACITY = 4
        B, T, D = x.shape
        E = w_key.shape[0]
        N = B * T
        C = max(MIN_CAPACITY, N // E)
        xprev = jnp.concatenate([shift_state[:, None, :], x[:, :-1]], axis=1)
        dxprev = xprev - x
        xk = x + dxprev * time_maa_k
        xr = x + dxprev * time_maa_r
        e_idx = token_ids.reshape(N).astype(jnp.int32) * HASH_PRIME % E
        onehot = (e_idx[:, None] == jnp.arange(E, dtype=jnp.int32)[None, :]).astype(jnp.int32)
        pos = jnp.take_along_axis(jnp.cumsum(onehot, axis=0), e_idx[:, None], axis=1)[:, 0] - 1
        keep = pos < C
        slot = jnp.where(keep, e_idx * C + pos, E * C)
        xk_flat = xk.reshape(N, D)
        buf = jnp.zeros((E * C + 1, D), dtype=x.dtype).at[slot].set(xk_flat)
        expert_in = buf[:E * C].reshape(E, C, D)
        h = jnp.square(jax.nn.relu(jnp.einsum('ecd,edf->ecf', expert_in, w_key)))
        expert_out = jnp.einsum('ecf,efd->ecd', h, w_value)
        out_pad = jnp.concatenate([expert_out.reshape(E * C, D), jnp.zeros((1, D), dtype=x.dtype)], axis=0)
        y = out_pad[slot].reshape(B, T, D)
        r = jax.nn.sigmoid(jnp.einsum('btd,ed->bte', xr, w_recept))
        return r * y

    def _L2_cond_ref(video, seq, W_z, U_z, C_z, b_z, W_r, U_r, C_r, b_r, W, U, C, b):
        import jax, jax.numpy as jnp
        import numpy as np
        B, T, D_IN, V_IN, E = (64, 128, 512, 512, 512)
        vz = video @ C_z + b_z
        vr = video @ C_r + b_r
        vh = video @ C + b
        xz = jnp.einsum('btd,de->bte', seq, W_z)
        xr = jnp.einsum('btd,de->bte', seq, W_r)
        xh = jnp.einsum('btd,de->bte', seq, W)

        def step(h, xs):
            xzt, xrt, xht = xs
            z = jax.nn.sigmoid(xzt + h @ U_z + vz)
            r = jax.nn.sigmoid(xrt + h @ U_r + vr)
            hh = jnp.tanh(xht + r * h @ U + vh)
            h_new = (1.0 - z) * h + z * hh
            return (h_new, h_new)
        h0 = jnp.zeros((seq.shape[0], U.shape[0]), seq.dtype)
        xs = (jnp.swapaxes(xz, 0, 1), jnp.swapaxes(xr, 0, 1), jnp.swapaxes(xh, 0, 1))
        _, out_t = jax.lax.scan(step, h0, xs)
        return jnp.swapaxes(out_t, 0, 1)

    def _L3_cond_ref(x, ada_emb, base_layer, w1, b1, w2, b2, ln_g, ln_b):
        import jax, jax.numpy as jnp
        import numpy as np
        B, T, D = (128, 32, 512)
        ADA, INTER, RANK = (512, 512, 8)
        LN_EPS = 1e-05

        def _layernorm(x, g, b):
            mu = jnp.mean(x, axis=-1, keepdims=True)
            var = jnp.var(x, axis=-1, keepdims=True)
            return (x - mu) * jax.lax.rsqrt(var + LN_EPS) * g + b
        b, t, d = x.shape
        ae = _layernorm(ada_emb, ln_g, ln_b)
        h = jax.nn.gelu(ae @ w1 + b1, approximate=False)
        xw = h @ w2 + b2
        x_a, x_b = jnp.split(xw, 2, axis=-1)
        x_a = x_a.reshape(b, d, RANK)
        x_b = x_b.reshape(b, d, RANK)
        layer = base_layer[None, :, :] + jnp.einsum('bdr,bkr->bdk', x_a, x_b)
        out = jnp.einsum('btc,bco->bto', x, layer)
        return x + out
    x = x + _L0_cond_ref(cond_1024, x, L0_cond_W, L0_cond_b, L0_cond_alpha)
    x = x + _L1_cond_ref(x, itok_BxS_2_50255, cond_1024, L1_cond_time_maa_k, L1_cond_time_maa_r, L1_cond_w_recept, L1_cond_w_key, L1_cond_w_value)
    x = x + _L2_cond_ref(cond_1024, x, L2_cond_W_z, L2_cond_U_z, L2_cond_C_z, L2_cond_b_z, L2_cond_W_r, L2_cond_U_r, L2_cond_C_r, L2_cond_b_r, L2_cond_W, L2_cond_U, L2_cond_C, L2_cond_b)
    x = x + _L3_cond_ref(x, cond_1024, L3_cond_base_layer, L3_cond_w1, L3_cond_b1, L3_cond_w2, L3_cond_b2, L3_cond_ln_g, L3_cond_ln_b)
    return x

_drawn_inputs = setup_inputs


def setup_inputs(seed=0):
    import zlib

    import numpy as np

    out = dict(_drawn_inputs(seed))
    spreads = {'L0_cond_alpha': (0.10000000149011612, 0.6),
     'L2_cond_b_z': (0.0, 0.8),
     'L2_cond_b_r': (0.0, 2.0),
     'L2_cond_b': (0.0, 0.1),
     'L3_cond_b1': (0.0, 0.502),
     'L3_cond_b2': (0.0, 0.1),
     'L3_cond_ln_g': (1.0, 0.6),
     'L3_cond_ln_b': (0.0, 0.8)}
    factors = {'L0_cond_b': 28.577,
     'L1_cond_time_maa_r': 6.711,
     'L1_cond_w_recept': 2.754,
     'L2_cond_W_z': 3.1,
     'L2_cond_U_z': 8.0,
     'L2_cond_C_z': 5.102,
     'L2_cond_W_r': 8.0,
     'L2_cond_U_r': 57.878,
     'L2_cond_C_r': 8.0,
     'L2_cond_U': 3.094}
    for name, (base, spread) in spreads.items():
        noise = np.random.default_rng([zlib.crc32(name.encode()), seed]).standard_normal(out[name].shape)
        drawn = base * np.exp(spread * noise) if base else spread * noise
        out[name] = jnp.asarray(drawn.astype(out[name].dtype))
    for name, factor in factors.items():
        out[name] = (out[name] * factor).astype(out[name].dtype)
    return out
```

```python
import concourse.bass as bass
from concourse import mybir
from contextlib import ExitStack

F32 = mybir.dt.float32
BF16 = mybir.dt.bfloat16
I32 = mybir.dt.int32
ALU = mybir.AluOpType
ACT = mybir.ActivationFunctionType
AX_X = mybir.AxisListType.X

P = 128
B = 2
T = 2048
D = 512
NG = 4
KC = D // P
S = KC * B
TC = 256
NCH = T // TC
TOKC = TC * B
U = 32
HB = U // 2
NBLK = TC // U
E = 16
F = 1024
FC = F // P
CAP = B * T // E
SC = CAP // P
NTOK = B * T
NT = NTOK // P
TPC = TOKC // P
TH = TC // P
RANK = 8
LN_EPS = 1e-5
NPIECE = 2 * D * RANK // D
HASH = 5099 % E


def steps8(t, n):
    return t[:, n * S:(n + 1) * S]


def grouped(t):
    return t.rearrange("p (c b) -> p c b", b=B)


def turned(t):
    return t[:, 0:P].rearrange("p (c r) -> p c r", c=KC)[:, :, 0:B]


def wait_alone(k, engine, sem, value):
    engine.wait_ge(sem, value)
    engine.sem_inc(k.passed, 1)


def matvec(pe, bank, w, h):
    for k in range(KC):
        for j in range(NG):
            last = pe.matmul(bank[32 * j:32 * j + B, 0:P], h[:, k, :], w[:, k, j * P:(j + 1) * P],
                             start=(k == 0), stop=(k == KC - 1), tile_position=(0, 32 * j),
                             skip_group_check=True)
    return last


def chunk_steps(a, c, shift=1):
    return a[:, bass.ds(c * (TC * S) + shift * S, TC * S)].rearrange("p (t c b) -> p t c b", c=KC, b=B)


def conditioning(nc, k, dram):
    with ExitStack() as ctx:
        sb = lambda n, s, d=F32: ctx.enter_context(nc.sbuf_tensor(n, s, d))
        sem = lambda n: ctx.enter_context(nc.semaphore(n))
        cw = sb("cond_w", [P, 3, KC, KC, P])
        w1 = sb("ada_w1", [P, KC, KC, P])
        w2 = sb("ada_w2", [P, 2, KC, D])
        b2 = sb("ada_b2", [B, 2, D])
        xw = sb("ada_xw", [B, 2, D])
        lnb = sb("ln_gb1", [P, 3, KC])
        low = sb("low_rank", [RANK, 2, B, D])
        base = sb("base", [P, KC, D])
        ones = sb("ones", [P, P])
        cen = sb("centred", [P, S])
        sq = sb("squares", [P, S])
        st = sb("stats", [P, 8])
        ae = sb("ada", [P, S])
        hp = sb("hidden_pre", [P, S])
        hid = sb("hidden", [P, S])
        loads, loads2, low_loaded = sem("c_loads"), sem("c_base"), sem("c_low")
        w2_in = [sem("c_w2_even"), sem("c_w2_odd")]
        xw_ps, xw_ready = sem("c_xw_ps"), sem("c_xw_ready")
        xw_out = [sem("c_xw_out_even"), sem("c_xw_out_odd")]
        v, pes, acts, lowps, lowuse = sem("c_dve"), sem("c_pe"), sem("c_act"), sem("c_lowps"), sem("c_lowuse")
        bank = k.banks
        block = ctx.enter_context(nc.Block())

        @block.sync
        def _(sp):
            sp.dma_start(k.A[:, 0:S], dram["cond"]).then_inc(loads, 16)
            sp.dma_start(lnb[:], dram["lnb"]).then_inc(loads, 16)
            sp.dma_start(k.bgru[:], dram["bgru"]).then_inc(loads, 16)
            sp.dma_start(w1[:], dram["w1"]).then_inc(loads, 16)
            for g in range(3):
                sp.dma_start(cw[:, g], dram["cg"][g]).then_inc(loads, 16)
            with sp.Fori(0, NPIECE // 2) as i:
                for s in range(2):
                    sp.wait_ge(xw_ready, 2 * i + s + 1)
                    sp.dma_start(w2[:, s], dram["w2"][:, bass.ds(2 * i + s, 1)].rearrange("p o k n -> p (o k) n")).then_inc(w2_in[s], 16)
                    sp.dma_start(b2[:, s], dram["b2"][:, bass.ds((2 * i + s) * D, D)]).then_inc(w2_in[s], 16)
            sp.dma_start(base[:], dram["base"]).then_inc(loads2, 16)
            for c in range(NCH):
                sp.dma_start(k.A[:, S + c * TC * S:S + (c + 1) * TC * S],
                             dram["x"][:, c * TC * S:(c + 1) * TC * S]).then_inc(k.x_loaded, 16)
            sp.wait_ge(xw_out[0], 16 * (NPIECE // 2) + 16)
            sp.wait_ge(xw_out[1], 16 * (NPIECE // 2) + 16)
            for h in range(2):
                for b in range(B):
                    sp.dma_start(low[:, h, b, :], dram["xw"][b, h * RANK:(h + 1) * RANK, :]).then_inc(low_loaded, 16)

        @block.vector
        def _(dve):
            n = [0]

            def step(ins):
                n[0] += 1
                ins.then_inc(v, 1)
                dve.wait_ge(v, n[0])

            dve.sem_inc(xw_ready, 2)
            step(dve.memset(ones[:], 1.0))
            dve.wait_ge(loads, 16 * 7)
            dve.wait_ge(pes, 1)
            step(dve.tensor_copy(st[:, 0:2], bank[0][:, 0:2]))
            step(dve.tensor_scalar(st[:, 2:4], st[:, 0:2], 1.0 / D, None, ALU.mult))
            for b in range(B):
                step(dve.tensor_scalar(grouped(cen[:])[:, :, b], grouped(k.A[:, 0:S])[:, :, b], st[:, 2 + b:3 + b], None, ALU.subtract))
            step(dve.tensor_tensor(sq[:], cen[:], cen[:], ALU.mult))
            dve.wait_ge(pes, 2)
            step(dve.tensor_scalar(st[:, 4:6], bank[1][:, 0:2], 1.0 / D, LN_EPS, ALU.mult, ALU.add))
            dve.wait_ge(acts, 1)
            step(dve.reciprocal(st[:, 6:8], st[:, 0:2]))
            for b in range(B):
                step(dve.tensor_scalar(grouped(ae[:])[:, :, b], grouped(cen[:])[:, :, b], st[:, 6 + b:7 + b], None, ALU.mult))
            for b in range(B):
                step(dve.tensor_tensor(grouped(ae[:])[:, :, b], grouped(ae[:])[:, :, b], lnb[:, 0, :], ALU.mult))
            for b in range(B):
                step(dve.tensor_tensor(grouped(ae[:])[:, :, b], grouped(ae[:])[:, :, b], lnb[:, 1, :], ALU.add))
            for g in range(3):
                dve.wait_ge(pes, 3 + g)
                for b in range(B):
                    step(dve.tensor_tensor(grouped(k.vg[:, g])[:, :, b], grouped(bank[2 + g][:, 0:S])[:, :, b], k.bgru[:, g, :], ALU.add))
            dve.wait_ge(pes, 6)
            for b in range(B):
                step(dve.tensor_tensor(grouped(hp[:])[:, :, b], grouped(bank[5][:, 0:S])[:, :, b], lnb[:, 2, :], ALU.add))
            with dve.Fori(0, NPIECE // 2) as i:
                for s in range(2):
                    dve.wait_ge(xw_ps, 2 * i + s + 3)
                    dve.wait_ge(xw_out[s], 16 * i + 16)
                    dve.tensor_tensor(xw[:, s], bank[6 + s][0:B, :], b2[:, s], ALU.add).then_inc(xw_ready, 1)
            dve.wait_ge(loads2, 16)
            for b in range(B):
                for c in range(KC):
                    dve.wait_ge(lowps, b * KC + c + 1)
                    dve.tensor_tensor(k.layer[:, b, c, :], base[:, c, :], bank[(b * KC + c) % 2][:, :], ALU.add).then_inc(lowuse, 1)
            dve.wait_ge(lowuse, B * KC)

        @block.scalar
        def _(act):
            act.wait_ge(v, 7)
            act.activation(st[:, 0:2], st[:, 4:6], ACT.Sqrt).then_inc(acts, 1)
            act.wait_ge(v, 22)
            act.activation(hid[:], hp[:], ACT.Gelu).then_inc(acts, 1)
            act.sem_inc(xw_out[0], 16)
            act.sem_inc(xw_out[1], 16)
            with act.Fori(0, NPIECE // 2) as i:
                for s in range(2):
                    act.wait_ge(xw_ready, 2 * i + s + 3)
                    act.dma_start(dram["xw"][:, bass.ds(2 * i + s, 1), :].rearrange("b o n -> b (o n)"), xw[:, s]).then_inc(xw_out[s], 16)

        @block.tensor
        def _(pe):
            def over_features(out, lhs, rhs):
                for c in range(KC):
                    last = pe.matmul(out, lhs(c), rhs(c), start=(c == 0), stop=(c == KC - 1))
                return last

            pe.sem_inc(xw_ps, 2)
            pe.wait_ge(v, 1)
            pe.wait_ge(loads, 16 * 7)
            cond = grouped(k.A[:, 0:S])
            over_features(bank[0][:, 0:2], lambda c: ones[:], lambda c: cond[:, c, :]).then_inc(pes, 1)
            pe.wait_ge(v, 6)
            over_features(bank[1][:, 0:2], lambda c: ones[:], lambda c: grouped(sq[:])[:, c, :]).then_inc(pes, 1)
            for g in range(3):
                for o in range(KC):
                    last = over_features(bank[2 + g][:, o * B:(o + 1) * B], lambda c: cw[:, g, c, o, :], lambda c: cond[:, c, :])
                last.then_inc(pes, 1)
            pe.wait_ge(v, 14)
            for o in range(KC):
                last = over_features(bank[5][:, o * B:(o + 1) * B], lambda c: w1[:, c, o, :], lambda c: grouped(ae[:])[:, c, :])
            last.then_inc(pes, 1)
            pe.wait_ge(acts, 2)
            with pe.Fori(0, NPIECE // 2) as i:
                for s in range(2):
                    pe.wait_ge(w2_in[s], 32 * i + 32)
                    pe.wait_ge(xw_ready, 2 * i + s + 1)
                    over_features(bank[6 + s][0:B, :], lambda c: grouped(hid[:])[:, c, :], lambda c: w2[:, s, c, :]).then_inc(xw_ps, 1)
            pe.wait_ge(low_loaded, 64)
            for b in range(B):
                for c in range(KC):
                    n = b * KC + c
                    if n >= 2:
                        pe.wait_ge(lowuse, n - 1)
                    pe.matmul(bank[n % 2][:, :], low[:, 0, b, c * P:(c + 1) * P], low[:, 1, b, :], start=True, stop=True).then_inc(lowps, 1)


def routing(nc, k, dram):
    with ExitStack() as ctx:
        sb = lambda n, s, d=F32: ctx.enter_context(nc.sbuf_tensor(n, s, d))
        sem = lambda n: ctx.enter_context(nc.semaphore(n))
        tok = sb("tok", [P, NT], I32)
        ei = sb("expert_i", [P, NT], I32)
        ef = sb("expert", [P, NT])
        iota_e = sb("iota_e", [P, E], I32)
        iota_n = sb("iota_n", [P, NT], I32)
        iota_ef = sb("iota_ef", [P, E])
        trash = sb("trash", [P, NT])
        hot = sb("one_hot", [P, NT, E])
        tot = sb("totals", [P, NT, E])
        run = [sb("run_a", [P, NT, E]), sb("run_b", [P, NT, E])]
        pos = sb("pos", [P, NT])
        keep = sb("keep", [P, NT])
        slot = sb("slot", [P, NT])
        dif = sb("dif", [P, NT])
        upto = sb("upto", [P, P])
        ones = sb("r_ones", [P, P])
        zeros = sb("r_zeros", [P, D])
        tok_in, made, v, counted, zero_out = sem("r_tok"), sem("r_made"), sem("r_dve"), sem("r_counted"), sem("r_zero_out")
        block = ctx.enter_context(nc.Block())

        @block.sync
        def _(sp):
            sp.dma_start(tok[:], dram["tok"]).then_inc(tok_in, 16)
            sp.wait_ge(made, 6)
            for n in range(E * SC):
                sp.dma_start(dram["expert_in"][n * P:(n + 1) * P, :], zeros[:]).then_inc(zero_out, 16)
            sp.dma_start(dram["expert_out"][E * CAP:E * CAP + 1, :], zeros[0:1, :]).then_inc(zero_out, 16)
            sp.wait_ge(zero_out, 16 * (E * SC + 1))

        @block.gpsimd
        def _(pool):
            pool.iota(iota_e[:], pattern=[[1, E]], base=0, channel_multiplier=0).then_inc(made, 1)
            pool.iota(iota_n[:], pattern=[[P, NT]], base=E * CAP, channel_multiplier=1).then_inc(made, 1)
            pool.memset(upto[:], 1.0).then_inc(made, 1)
            pool.memset(k.ident[:], 0.0).then_inc(made, 1)
            pool.memset(ones[:], 1.0).then_inc(made, 1)
            pool.memset(zeros[:], 0.0).then_inc(made, 1)
            pool.wait_ge(made, 6)
            pool.affine_select(out=upto[:], in_=upto[:], pattern=[[1, P]], compare_op=ALU.is_ge, fill=0.0, base=0, channel_multiplier=-1).then_inc(made, 1)
            pool.affine_select(out=k.ident[:], in_=k.ident[:], pattern=[[-1, P]], compare_op=ALU.not_equal, fill=1.0, base=0, channel_multiplier=1).then_inc(made, 1)

        @block.vector
        def _(dve):
            n = [0]

            def step(ins):
                n[0] += 1
                ins.then_inc(v, 1)
                dve.wait_ge(v, n[0])

            dve.wait_ge(tok_in, 16)
            dve.wait_ge(made, 6)
            step(dve.tensor_scalar(ei[:], tok[:], E - 1, None, ALU.bitwise_and))
            step(dve.tensor_scalar(ei[:], ei[:], HASH, None, ALU.mult))
            step(dve.tensor_scalar(ei[:], ei[:], E - 1, None, ALU.bitwise_and))
            step(dve.tensor_copy(ef[:], ei[:]))
            step(dve.tensor_copy(iota_ef[:], iota_e[:]))
            step(dve.tensor_copy(trash[:], iota_n[:]))
            step(dve.tensor_tensor(hot[:], ef[:].unsqueeze(2).to_broadcast([P, NT, E]), iota_ef[:].unsqueeze(1).to_broadcast([P, NT, E]), ALU.is_equal))
            dve.wait_ge(counted, 1)
            step(dve.tensor_copy(tot[:].rearrange("p n e -> p (n e)"), k.banks[1][:, :]))
            step(dve.tensor_copy(run[0][:], tot[:]))
            a = 0
            d = 1
            while d < NT:
                step(dve.tensor_copy(run[1 - a][:, 0:d], run[a][:, 0:d]))
                step(dve.tensor_tensor(run[1 - a][:, d:NT], run[a][:, d:NT], run[a][:, 0:NT - d], ALU.add))
                a = 1 - a
                d *= 2
            step(dve.tensor_tensor(tot[:], run[a][:], tot[:], ALU.subtract))
            step(dve.tensor_tensor(tot[:], tot[:], k.banks[0][:, :].rearrange("p (n e) -> p n e", e=E), ALU.add))
            step(dve.tensor_tensor(tot[:], tot[:], hot[:], ALU.mult))
            step(dve.tensor_reduce(pos[:], tot[:], AX_X, ALU.add))
            step(dve.tensor_scalar(keep[:], pos[:], float(CAP), None, ALU.is_le))
            step(dve.tensor_scalar(slot[:], ef[:], float(CAP), -1.0, ALU.mult, ALU.add))
            step(dve.tensor_tensor(slot[:], slot[:], pos[:], ALU.add))
            step(dve.tensor_tensor(dif[:], slot[:], trash[:], ALU.subtract))
            step(dve.tensor_tensor(dif[:], dif[:], keep[:], ALU.mult))
            step(dve.tensor_tensor(dif[:], dif[:], trash[:], ALU.add))
            step(dve.tensor_copy(k.put[:], dif[:]))
            step(dve.tensor_scalar(slot[:], slot[:], -float(E * CAP), None, ALU.add))
            step(dve.tensor_tensor(slot[:], slot[:], keep[:], ALU.mult))
            step(dve.tensor_scalar(slot[:], slot[:], float(E * CAP), None, ALU.add))
            step(dve.tensor_copy(k.get[:], slot[:]))

        @block.tensor
        def _(pe):
            pe.wait_ge(made, 8)
            pe.wait_ge(v, 7)
            flat = hot[:].rearrange("p n e -> p (n e)")
            pe.matmul(k.banks[0][:, :], upto[:], flat, start=True, stop=True)
            pe.matmul(k.banks[1][:, :], ones[:], flat, start=True, stop=True).then_inc(counted, 1)


def leaky_recurrence(nc, k, dram):
    with ExitStack() as ctx:
        sb = lambda n, s, d=F32: ctx.enter_context(nc.sbuf_tensor(n, s, d))
        sem = lambda n: ctx.enter_context(nc.semaphore(n))
        wh = sb("l0_wh", [P, KC, D])
        wz = sb("l0_wz", [P, KC, KC, P])
        vecs = sb("l0_b_alpha", [P, 2, KC])
        leak = sb("leak", [P, S])
        xz = sb("xz", [P, TC * S])
        xz_ring = sb("xz_ring", [P, U * S])
        x_ring = sb("x_ring", [P, U * S])
        h_ring = sb("h_ring", [P, U * S])
        warm = sb("warm", [P, D], BF16)
        hw_t = sb("hw_t", [P, P])
        pre, gate, gx, hl, u_ = (sb(n, [P, S]) for n in ("pre", "gate", "gate_x", "h_leak", "update"))
        loads, ready = sem("l0_loads"), sem("l0_ready")
        proj, projected = sem("l0_proj"), sem("l0_projected")
        staged, hw_ready, pre_ready, gate_ready, chain, h_ready, added = (sem("l0_" + n) for n in (
            "staged", "hw_ready", "pre_ready", "gate_ready", "chain", "h_ready", "added"))
        hw = k.banks[4]
        block = ctx.enter_context(nc.Block())

        @block.sync
        def _(sp):
            sp.dma_start(wh[:], dram["wh"]).then_inc(loads, 16)
            sp.dma_start(wz[:], dram["wz"]).then_inc(loads, 16)
            sp.dma_start(vecs[:], dram["l0v"]).then_inc(loads, 16)

        @block.tensor
        def _(pe):
            pe.wait_ge(loads, 48)
            pe.wait_ge(k.x_loaded, 16 * NCH)
            pe.wait_ge(ready, 1)
            with pe.Fori(0, NCH) as c:
                for o in range(KC):
                    for q in range(KC):
                        last = pe.matmul(k.banks[o][:, :], wz[:, q, o, :], chunk_steps(k.A, c)[:, :, q, :],
                                         start=(q == 0), stop=(q == KC - 1))
                    last.then_inc(proj, 1)
                with pe.Fori(0, NBLK) as i:
                    for u in range(U):
                        pe.wait_ge(h_ready, c * TC + i * U + u + 1)
                        matvec(pe, hw, wh, grouped(steps8(h_ring, (u - 1) % U))).then_inc(hw_ready, 1)
                        for _ in range(3):
                            pe.matmul(k.banks[5][0:B, :], warm[:, 0:B], warm[:, :], start=True, stop=True)

        @block.scalar
        def _(act):
            act.wait_ge(ready, 1)
            with act.Fori(0, NCH) as c:
                for o in range(KC):
                    act.wait_ge(proj, c * KC + o + 1)
                    act.activation(xz[:].rearrange("p (t c b) -> p t c b", c=KC, b=B)[:, :, o, :],
                                   k.banks[o][:, :].rearrange("p (t b) -> p t b", b=B),
                                   ACT.Identity, bias=vecs[:, 0, o:o + 1]).then_inc(projected, 1)
                with act.Fori(0, NBLK) as i:
                    for u in range(U):
                        st = c * TC + i * U + u
                        act.wait_ge(pre_ready, st + 1)
                        act.activation(gate[:], pre[:], ACT.Sigmoid).then_inc(gate_ready, 1)
                        act.wait_ge(chain, 4 * st + 4)
                        if u % HB == 0:
                            act.wait_ge(added, (c * NBLK + i) * 2 + u // HB + 1)
                        act.activation(steps8(h_ring, u), u_[:], ACT.Tanh).then_inc(h_ready, 1)

        @block.gpsimd
        def _(pool):
            pool.sem_inc(added, 2)
            with pool.Fori(0, NCH) as c:
                wait_alone(k, pool, projected, (c + 1) * KC)
                for half in range(2):
                    a, b = half * HB * S, (half + 1) * HB * S
                    pool.tensor_copy(xz_ring[:, a:b], xz[:, a:b]).then_inc(staged, 1)
                    pool.tensor_copy(x_ring[:, a:b], k.A[:, bass.ds(S + c * (TC * S) + a, HB * S)]).then_inc(staged, 1)
                with pool.Fori(0, NBLK - 1) as i:
                    for half in range(2):
                        a, b = half * HB * S, (half + 1) * HB * S
                        at = i * (U * S) + a
                        pool.wait_ge(h_ready, c * TC + i * U + (half + 1) * HB + 1)
                        here = k.A[:, bass.ds(S + c * (TC * S) + at, HB * S)]
                        pool.tensor_tensor(here, here, h_ring[:, a:b], ALU.add).then_inc(added, 1)
                        pool.tensor_copy(xz_ring[:, a:b], xz[:, bass.ds(at + U * S, HB * S)]).then_inc(staged, 1)
                        pool.tensor_copy(x_ring[:, a:b], k.A[:, bass.ds(S + U * S + c * (TC * S) + at, HB * S)]).then_inc(staged, 1)
                for half in range(2):
                    a, b = half * HB * S, (half + 1) * HB * S
                    pool.wait_ge(h_ready, c * TC + (NBLK - 1) * U + (half + 1) * HB + 1)
                    here = k.A[:, bass.ds(S + c * (TC * S) + (NBLK - 1) * U * S + a, HB * S)]
                    pool.tensor_tensor(here, here, h_ring[:, a:b], ALU.add).then_inc(added, 1)

        @block.vector
        def _(dve):
            dve.wait_ge(loads, 48)
            for b in range(B):
                dve.tensor_scalar(grouped(leak[:])[:, :, b], vecs[:, 1, :], -1.0, 1.0, ALU.mult, ALU.add)
            dve.memset(warm[:], 0.0)
            dve.memset(hw[:, 0:P], 0.0)
            dve.tensor_copy(steps8(h_ring, U - 1), k.A[:, 0:S]).then_inc(h_ready, 1)
            dve.wait_ge(h_ready, 1)
            dve.memset(gate[:], 0.0).then_inc(ready, 1)
            dve.wait_ge(ready, 1)
            with dve.Fori(0, NCH) as c:
                with dve.Fori(0, NBLK) as i:
                    for u in range(U):
                        st = c * TC + i * U + u
                        if u % HB == 0:
                            dve.wait_ge(staged, (c * NBLK + i) * 4 + 2 * (u // HB) + 2)
                        dve.wait_ge(h_ready, st + 1)
                        dve.tensor_tensor(hl[:], steps8(h_ring, (u - 1) % U), leak[:], ALU.mult).then_inc(chain, 1)
                        dve.wait_ge(hw_ready, st + 1)
                        dve.transpose(hw_t[:], hw[:, 0:P]).then_inc(chain, 1)
                        dve.wait_ge(chain, 4 * st + 2)
                        dve.tensor_tensor(grouped(pre[:]), turned(hw_t), grouped(steps8(xz_ring, u)), ALU.add).then_inc(pre_ready, 1)
                        dve.wait_ge(gate_ready, st + 1)
                        dve.tensor_tensor(gx[:], gate[:], steps8(x_ring, u), ALU.mult).then_inc(chain, 1)
                        dve.wait_ge(chain, 4 * st + 3)
                        dve.tensor_tensor(u_[:], gx[:], hl[:], ALU.add).then_inc(chain, 1)


def experts(nc, k, dram):
    with ExitStack() as ctx:
        sb = lambda n, s, d=F32: ctx.enter_context(nc.sbuf_tensor(n, s, d))
        sem = lambda n: ctx.enter_context(nc.semaphore(n))
        maa = sb("maa", [P, 2, KC])
        key = [sb(f"w_key{s}", [P, KC, FC, P]) for s in range(2)]
        val = [sb(f"w_value{s}", [P, FC, D]) for s in range(2)]
        w_in = [sem(f"m_w_in{s}") for s in range(2)]
        maa_in, shifted, mixed, rows_t, rows_ready, idx_ready, scattered, rows_free = (sem("m_" + n) for n in (
            "maa_in", "shifted", "mixed", "rows_t", "rows_ready", "idx_ready", "scattered", "rows_free"))
        with ExitStack() as c1:
            dx = c1.enter_context(nc.sbuf_tensor("dx", [P, TC, KC, B], F32))
            xk = c1.enter_context(nc.sbuf_tensor("xk", [P, KC, B, TC], F32))
            rows = c1.enter_context(nc.sbuf_tensor("rows", [P, TPC, D], F32))
            put = [c1.enter_context(nc.sbuf_tensor(f"put{n}", [P, 1], I32)) for n in range(TPC)]
            block = c1.enter_context(nc.Block())

            @block.sync
            def _(sp):
                sp.dma_start(maa[:], dram["maa"]).then_inc(maa_in, 16)
                for s in range(2):
                    sp.dma_start(key[s][:], dram["w_key"][s]).then_inc(w_in[s], 16)
                    sp.dma_start(val[s][:], dram["w_value"][s]).then_inc(w_in[s], 16)

            @block.vector
            def _(dve):
                dve.wait_ge(maa_in, 16)
                dve.sem_inc(mixed, 1)
                with dve.Fori(0, NCH) as c:
                    dve.tensor_tensor(dx[:], chunk_steps(k.A, c, 0), chunk_steps(k.A, c), ALU.subtract).then_inc(shifted, 1)
                    dve.wait_ge(shifted, c + 1)
                    dve.wait_ge(rows_t, c * TPC + TPC)
                    for o in range(KC):
                        last = dve.scalar_tensor_tensor(xk[:, o].rearrange("p b t -> p t b"), dx[:, :, o, :], maa[:, 0, o:o + 1],
                                                 chunk_steps(k.A, c)[:, :, o, :], ALU.mult, ALU.add)
                    last.then_inc(mixed, 1)
                    dve.wait_ge(mixed, c + 2)
                    wait_alone(k, dve, rows_free, c + 1)
                    for n in range(TPC):
                        last = dve.tensor_copy(put[n][:], k.put[:, bass.ds(c * TH + (n // TH) * (NT // B) + n % TH, 1)])
                    last.then_inc(idx_ready, 1)

            @block.tensor
            def _(pe):
                pe.sem_inc(rows_t, TPC)
                with pe.Fori(0, NCH) as c:
                    pe.wait_ge(mixed, c + 2)
                    for n in range(TPC):
                        pe.wait_ge(rows_ready, c * TPC + n + 1)
                        for o in range(KC):
                            last = pe.transpose(k.banks[n][:, o * P:(o + 1) * P], xk[:, o, n // TH, (n % TH) * P:(n % TH + 1) * P], k.ident[:])
                        last.then_inc(rows_t, 1)

            @block.scalar
            def _(act):
                act.sem_inc(rows_ready, TPC)
                with act.Fori(0, NCH) as c:
                    act.wait_ge(rows_free, c + 1)
                    for n in range(TPC):
                        act.wait_ge(rows_t, c * TPC + n + 1 + TPC)
                        act.activation(rows[:, n, :], k.banks[n][:, :], ACT.Copy).then_inc(rows_ready, 1)

            @block.gpsimd
            def _(pool):
                pool.sem_inc(rows_free, 1)
                with pool.Fori(0, NCH) as c:
                    pool.wait_ge(idx_ready, c + 1)
                    for n in range(TPC):
                        wait_alone(k, pool, rows_ready, c * TPC + n + 1 + TPC)
                        pool.indirect_dma_start(out=dram["expert_in"][:, :], out_offset=bass.IndirectOffsetOnAxis(ap=put[n][:, 0:1], axis=0),
                                                in_=rows[:, n, :], in_offset=None).then_inc(scattered, 16)
                    pool.wait_ge(scattered, 16 * TPC * (c + 1))
                    pool.sem_inc(rows_free, 1)

        with ExitStack() as c2:
            xin = [c2.enter_context(nc.sbuf_tensor(f"xin{s}", [P, SC, D], F32)) for s in range(2)]
            xt = c2.enter_context(nc.sbuf_tensor("xt", [P, KC, CAP], F32))
            rel = [c2.enter_context(nc.sbuf_tensor(f"relu{s}", [P, CAP], F32)) for s in range(2)]
            hid = c2.enter_context(nc.sbuf_tensor("hid", [P, FC, CAP], F32))
            yo = c2.enter_context(nc.sbuf_tensor("yo", [P, SC, D], F32))
            x_in = [c2.enter_context(nc.semaphore(f"m_x_in{s}")) for s in range(2)]
            turned_ps, xt_ready, key_ps, rel_ready, hid_ready, val_ps, yo_ready, y_out = (
                c2.enter_context(nc.semaphore("m_" + n)) for n in (
                    "turned_ps", "xt_ready", "key_ps", "rel_ready", "hid_ready", "val_ps", "yo_ready", "y_out"))
            block = c2.enter_context(nc.Block())

            @block.sync
            def _(sp):
                for s in range(2):
                    sp.dma_start(xin[s][:], dram["expert_in"][s * CAP:(s + 1) * CAP, :].rearrange("(s p) d -> p s d", p=P)).then_inc(x_in[s], 16)
                with sp.Fori(0, E // 2 - 1) as i:
                    for s in range(2):
                        sp.wait_ge(val_ps, (2 * i + s + 2) * SC)
                        nxt = 2 * i + s + 2
                        sp.dma_start(key[s][:], dram["w_key"][bass.ds(nxt, 1)].rearrange("e p a b c -> (e p) a b c")).then_inc(w_in[s], 16)
                        sp.dma_start(val[s][:], dram["w_value"][bass.ds(nxt, 1)].rearrange("e p a b -> (e p) a b")).then_inc(w_in[s], 16)
                        sp.dma_start(xin[s][:], dram["expert_in"][bass.ds(nxt * CAP, CAP), :].rearrange("(s p) d -> p s d", p=P)).then_inc(x_in[s], 16)

            @block.tensor
            def _(pe):
                pe.sem_inc(key_ps, FC)
                pe.sem_inc(val_ps, SC)
                with pe.Fori(0, E // 2) as i:
                    for s in range(2):
                        e = 2 * i + s
                        pe.wait_ge(x_in[s], 16 * i + 16)
                        pe.wait_ge(xt_ready, e * SC + SC)
                        for h in range(SC):
                            for o in range(KC):
                                last = pe.transpose(k.banks[h][:, o * P:(o + 1) * P], xin[s][:, h, o * P:(o + 1) * P], k.ident[:])
                            last.then_inc(turned_ps, 1)
                        pe.wait_ge(w_in[s], 32 * i + 32)
                        pe.wait_ge(xt_ready, e * SC + 2 * SC)
                        for f in range(FC):
                            pe.wait_ge(rel_ready, e * FC + f + 1)
                            for o in range(KC):
                                last = pe.matmul(k.banks[2 + f % 2][:, 0:CAP], key[s][:, o, f, :], xt[:, o, :], start=(o == 0), stop=(o == KC - 1))
                            last.then_inc(key_ps, 1)
                        pe.wait_ge(hid_ready, e * FC + FC + 2)
                        pe.wait_ge(yo_ready, e * SC + SC)
                        for h in range(SC):
                            for f in range(FC):
                                last = pe.matmul(k.banks[4 + h][:, :], hid[:, f, h * P:(h + 1) * P], val[s][:, f, :], start=(f == 0), stop=(f == FC - 1))
                            last.then_inc(val_ps, 1)

            @block.scalar
            def _(act):
                act.sem_inc(rel_ready, 2)
                with act.Fori(0, E) as e:
                    for f in range(FC):
                        act.wait_ge(key_ps, e * FC + f + 1 + FC)
                        act.wait_ge(hid_ready, e * FC + f + 1)
                        act.activation(rel[f % 2][:], k.banks[2 + f % 2][:, 0:CAP], ACT.Relu).then_inc(rel_ready, 1)
                    act.wait_ge(yo_ready, e * SC + 2 * SC)
                    act.dma_start(dram["expert_out"][bass.ds(e * CAP, CAP), :].rearrange("(s p) d -> p s d", p=P), yo[:]).then_inc(y_out, 16)
                act.wait_ge(y_out, 16 * (E + 1))

            @block.vector
            def _(dve):
                dve.sem_inc(xt_ready, SC)
                dve.sem_inc(hid_ready, 2)
                dve.sem_inc(yo_ready, SC)
                dve.sem_inc(y_out, 16)
                with dve.Fori(0, E) as e:
                    dve.wait_ge(key_ps, e * FC + FC)
                    for h in range(SC):
                        dve.wait_ge(turned_ps, e * SC + h + 1)
                        dve.tensor_copy(xt[:, :, h * P:(h + 1) * P], k.banks[h][:, :].rearrange("p (c t) -> p c t", c=KC)).then_inc(xt_ready, 1)
                    dve.wait_ge(val_ps, e * SC + SC)
                    for f in range(FC):
                        dve.wait_ge(rel_ready, e * FC + f + 1 + 2)
                        dve.tensor_tensor(hid[:, f, :], rel[f % 2][:], rel[f % 2][:], ALU.mult).then_inc(hid_ready, 1)
                    dve.wait_ge(y_out, 16 * e + 16)
                    for h in range(SC):
                        dve.wait_ge(val_ps, e * SC + h + 1 + SC)
                        dve.tensor_copy(yo[:, h, :], k.banks[4 + h][:, :]).then_inc(yo_ready, 1)


def combine(nc, k, dram):
    with ExitStack() as ctx:
        sb = lambda n, s, d=F32: ctx.enter_context(nc.sbuf_tensor(n, s, d))
        sem = lambda n: ctx.enter_context(nc.semaphore(n))
        maa = sb("maa_again", [P, 2, KC])
        wr = sb("w_recept", [P, KC, KC, P])
        dx = sb("dxr", [P, TC, KC, B])
        xr = sb("xr", [P, KC, TOKC])
        r = sb("recept", [P, KC, TC, B])
        get = [sb(f"get{n}", [P, 1], I32) for n in range(TPC)]
        y = sb("y_rows", [P, TPC, D])
        ry = sb("r_times_y", [P, TPC, KC, P])
        loads, shifted, mixed, r_ps, r_ready, idx_ready, yt_ps, mulled, added = (sem("g_" + n) for n in (
            "loads", "shifted", "mixed", "r_ps", "r_ready", "idx_ready", "yt_ps", "mulled", "added"))
        gathered = [sem(f"g_gathered{n}") for n in range(TPC)]
        block = ctx.enter_context(nc.Block())

        @block.sync
        def _(sp):
            sp.dma_start(maa[:], dram["maa"]).then_inc(loads, 16)
            sp.dma_start(wr[:], dram["w_recept"]).then_inc(loads, 16)

        @block.vector
        def _(dve):
            dve.wait_ge(loads, 32)
            dve.sem_inc(mulled, TPC)
            with dve.Fori(0, NCH) as i:
                c = (NCH - 1) - i
                wait_alone(k, dve, yt_ps, i * TPC + TPC)
                for n in range(TPC):
                    last = dve.tensor_copy(get[n][:], k.get[:, bass.ds(c * TH + (n // TH) * (NT // B) + n % TH, 1)])
                last.then_inc(idx_ready, 1)
                dve.tensor_tensor(dx[:], chunk_steps(k.A, c, 0), chunk_steps(k.A, c), ALU.subtract).then_inc(shifted, 1)
                dve.wait_ge(shifted, i + 1)
                dve.wait_ge(r_ps, i * KC + KC)
                for o in range(KC):
                    last = dve.scalar_tensor_tensor(xr[:, o].rearrange("p (t b) -> p t b", b=B), dx[:, :, o, :], maa[:, 1, o:o + 1],
                                                    chunk_steps(k.A, c)[:, :, o, :], ALU.mult, ALU.add)
                last.then_inc(mixed, 1)
                dve.wait_ge(r_ready, i * KC + 2 * KC)
                for n in range(TPC):
                    b, h = n // TH, n % TH
                    dve.wait_ge(yt_ps, i * TPC + n + 1 + TPC)
                    dve.tensor_tensor(ry[:, n], r[:, :, h * P:(h + 1) * P, b], k.banks[4 + n][:, :].rearrange("p (c t) -> p c t", c=KC), ALU.mult).then_inc(mulled, 1)
                    dve.wait_ge(mulled, i * TPC + n + 1 + TPC)
                    here = k.A[:, bass.ds(S + c * (TC * S) + h * (P * S), P * S)].rearrange("p (t c b) -> p c t b", c=KC, b=B)[:, :, :, b]
                    dve.tensor_tensor(here, here, ry[:, n], ALU.add).then_inc(added, 1)
                dve.wait_ge(added, (i + 1) * TPC)

        @block.tensor
        def _(pe):
            pe.wait_ge(loads, 32)
            pe.sem_inc(yt_ps, TPC)
            pe.sem_inc(r_ps, KC)
            with pe.Fori(0, NCH) as i:
                pe.wait_ge(mixed, i + 1)
                pe.wait_ge(r_ready, i * KC + KC)
                for o in range(KC):
                    for q in range(KC):
                        last = pe.matmul(k.banks[o][:, :], wr[:, q, o, :], xr[:, q, :], start=(q == 0), stop=(q == KC - 1))
                    last.then_inc(r_ps, 1)
                for n in range(TPC):
                    pe.wait_ge(gathered[n], 16 * i + 16)
                    pe.wait_ge(mulled, i * TPC + n + 1)
                    for o in range(KC):
                        last = pe.transpose(k.banks[4 + n][:, o * P:(o + 1) * P], y[:, n, o * P:(o + 1) * P], k.ident[:])
                    last.then_inc(yt_ps, 1)

        @block.scalar
        def _(act):
            act.sem_inc(r_ready, KC)
            with act.Fori(0, NCH) as i:
                act.wait_ge(mulled, i * TPC + TPC)
                for o in range(KC):
                    act.wait_ge(r_ps, i * KC + o + 1 + KC)
                    act.activation(r[:, o].rearrange("p t b -> p (t b)"), k.banks[o][:, :], ACT.Sigmoid).then_inc(r_ready, 1)

        @block.gpsimd
        def _(pool):
            with pool.Fori(0, NCH) as i:
                pool.wait_ge(idx_ready, i + 1)
                wait_alone(k, pool, yt_ps, i * TPC + TPC)
                for n in range(TPC):
                    pool.indirect_dma_start(out=y[:, n, :], out_offset=None, in_=dram["expert_out"][:, :],
                                            in_offset=bass.IndirectOffsetOnAxis(ap=get[n][:, 0:1], axis=0)).then_inc(gathered[n], 16)


def gru(nc, k, dram):
    Z, R, H = range(3)
    with ExitStack() as ctx:
        sb = lambda n, s, d=F32: ctx.enter_context(nc.sbuf_tensor(n, s, d))
        sem = lambda n: ctx.enter_context(nc.semaphore(n))
        ug = sb("gru_u", [P, 3, KC, D])
        wg = sb("gru_w", [P, 3, KC, KC, P])
        xg = sb("gru_x", [P, 3, TC * S])
        x_ring = sb("g_ring", [P, 3, U * S])
        h_ring = sb("gh_ring", [P, U * S])
        tz, tr, th = (sb(n, [P, P]) for n in ("hz_t", "hr_t", "hh_t"))
        pz, pr, ph, gz, gr, gh, rh, zh, keep = (sb(n, [P, S]) for n in (
            "pre_z", "pre_r", "pre_h", "gate_z", "gate_r", "cand", "rh", "z_cand", "keep_h"))
        loads, ready = sem("r_loads"), sem("r_ready")
        proj, projected, staged, added = (sem("r_" + n) for n in ("proj", "projected", "staged", "added"))
        r_ps, z_ps, h_ps, pre_r, pre_z, pre_h, r_gate, z_gate, cand, rh_ready, chain, h_ready = (sem("r_" + n) for n in (
            "r_ps", "z_ps", "h_ps", "pre_r", "pre_z", "pre_h", "r_gate", "z_gate", "cand", "rh_ready", "chain", "h_ready"))
        bz, br, bh = k.banks[4], k.banks[5], k.banks[6]
        block = ctx.enter_context(nc.Block())

        @block.sync
        def _(sp):
            for g in range(3):
                sp.dma_start(ug[:, g], dram["ug"][g]).then_inc(loads, 16)
                sp.dma_start(wg[:, g], dram["wg"][g]).then_inc(loads, 16)

        @block.tensor
        def _(pe):
            pe.wait_ge(loads, 96)
            pe.wait_ge(ready, 1)
            pe.sem_inc(proj, 4)
            with pe.Fori(0, NCH) as c:
                for g in range(3):
                    for o in range(KC):
                        pe.wait_ge(projected, c * (3 * KC) + g * KC + o + 1)
                        for q in range(KC):
                            last = pe.matmul(k.banks[o][:, :], wg[:, g, q, o, :], chunk_steps(k.A, c)[:, :, q, :],
                                             start=(q == 0), stop=(q == KC - 1))
                        last.then_inc(proj, 1)
                with pe.Fori(0, NBLK) as i:
                    for u in range(U):
                        st = c * TC + i * U + u
                        h = grouped(steps8(h_ring, (u - 1) % U))
                        pe.wait_ge(h_ready, st + 1)
                        matvec(pe, br, ug[:, R], h).then_inc(r_ps, 1)
                        matvec(pe, bz, ug[:, Z], h).then_inc(z_ps, 1)
                        pe.wait_ge(rh_ready, st + 1)
                        matvec(pe, bh, ug[:, H], grouped(rh[:])).then_inc(h_ps, 1)

        @block.scalar
        def _(act):
            act.wait_ge(ready, 1)
            act.sem_inc(projected, 4)
            with act.Fori(0, NCH) as c:
                act.wait_ge(added, 16 * c + 2)
                for g in range(3):
                    for o in range(KC):
                        act.wait_ge(proj, c * (3 * KC) + g * KC + o + 1 + 4)
                        for b in range(B):
                            last = act.activation(xg[:, g].rearrange("p (t c b) -> p t c b", c=KC, b=B)[:, :, o, b],
                                                  k.banks[o][:, :].rearrange("p (t b) -> p t b", b=B)[:, :, b],
                                                  ACT.Identity, bias=k.vg[:, g, o * B + b:o * B + b + 1])
                        last.then_inc(projected, 1)
                with act.Fori(0, NBLK) as i:
                    for u in range(U):
                        st = c * TC + i * U + u
                        act.wait_ge(pre_r, st + 1)
                        act.activation(gr[:], pr[:], ACT.Sigmoid).then_inc(r_gate, 1)
                        act.wait_ge(pre_z, st + 1)
                        act.activation(gz[:], pz[:], ACT.Sigmoid).then_inc(z_gate, 1)
                        act.wait_ge(pre_h, st + 1)
                        act.activation(gh[:], ph[:], ACT.Tanh).then_inc(cand, 1)

        @block.gpsimd
        def _(pool):
            pool.sem_inc(added, 2)
            with pool.Fori(0, NCH) as c:
                wait_alone(k, pool, projected, (c + 1) * (3 * KC) + 4)
                for half in range(2):
                    a, b = half * HB * S, (half + 1) * HB * S
                    pool.tensor_copy(x_ring[:, :, a:b], xg[:, :, a:b]).then_inc(staged, 1)
                with pool.Fori(0, NBLK - 1) as i:
                    for half in range(2):
                        a, b = half * HB * S, (half + 1) * HB * S
                        at = i * (U * S) + a
                        pool.wait_ge(h_ready, c * TC + i * U + (half + 1) * HB + 1)
                        here = k.A[:, bass.ds(S + c * (TC * S) + at, HB * S)]
                        pool.tensor_tensor(here, here, h_ring[:, a:b], ALU.add).then_inc(added, 1)
                        pool.tensor_copy(x_ring[:, :, a:b], xg[:, :, bass.ds(at + U * S, HB * S)]).then_inc(staged, 1)
                for half in range(2):
                    a, b = half * HB * S, (half + 1) * HB * S
                    pool.wait_ge(h_ready, c * TC + (NBLK - 1) * U + (half + 1) * HB + 1)
                    here = k.A[:, bass.ds(S + c * (TC * S) + (NBLK - 1) * U * S + a, HB * S)]
                    pool.tensor_tensor(here, here, h_ring[:, a:b], ALU.add).then_inc(added, 1)

        @block.vector
        def _(dve):
            for t in (bz, br, bh):
                dve.memset(t[:, 0:P], 0.0)
            dve.memset(steps8(h_ring, U - 1), 0.0).then_inc(h_ready, 1)
            dve.wait_ge(h_ready, 1)
            dve.memset(rh[:], 0.0).then_inc(ready, 1)
            dve.wait_ge(ready, 1)

            def pre_activation(bank, t, g, u, out, ps, st, links, done):
                dve.wait_ge(ps, st + 1)
                dve.transpose(t[:], bank[:, 0:P]).then_inc(chain, 1)
                dve.wait_ge(chain, 5 * st + links)
                dve.tensor_tensor(grouped(out[:]), turned(t), grouped(steps8(x_ring[:, g], u)), ALU.add).then_inc(done, 1)

            with dve.Fori(0, NCH) as c:
                with dve.Fori(0, NBLK) as i:
                    for u in range(U):
                        st = c * TC + i * U + u
                        h = steps8(h_ring, (u - 1) % U)
                        if u % HB == 0:
                            dve.wait_ge(staged, (c * NBLK + i) * 2 + (u // HB) + 1)
                            dve.wait_ge(added, (c * NBLK + i) * 2 + (u // HB) + 1)
                        pre_activation(br, tr, R, u, pr, r_ps, st, 1, pre_r)
                        dve.wait_ge(r_gate, st + 1)
                        dve.tensor_tensor(rh[:], gr[:], h, ALU.mult).then_inc(rh_ready, 1)
                        pre_activation(bz, tz, Z, u, pz, z_ps, st, 2, pre_z)
                        dve.wait_ge(z_gate, st + 1)
                        dve.scalar_tensor_tensor(keep[:], gz[:], -1.0, h, ALU.add, ALU.mult).then_inc(chain, 1)
                        pre_activation(bh, th, H, u, ph, h_ps, st, 4, pre_h)
                        dve.wait_ge(cand, st + 1)
                        dve.tensor_tensor(zh[:], gz[:], gh[:], ALU.mult).then_inc(chain, 1)
                        dve.wait_ge(chain, 5 * st + 5)
                        dve.tensor_tensor(steps8(h_ring, u), zh[:], keep[:], ALU.subtract).then_inc(h_ready, 1)


def adapted_output(nc, k, dram, out):
    with ExitStack() as ctx:
        sem = lambda n: ctx.enter_context(nc.semaphore(n))
        o_sb = [ctx.enter_context(nc.sbuf_tensor(f"out_sb{s}", [P, TC * S], F32)) for s in range(2)]
        out_ps, out_ready = sem("o_ps"), sem("o_ready")
        stored = [sem("o_stored0"), sem("o_stored1")]
        block = ctx.enter_context(nc.Block())

        @block.tensor
        def _(pe):
            with pe.Fori(0, NCH) as c:
                for o in range(KC):
                    pe.wait_ge(out_ready, c * KC + o + 1)
                    for b in range(B):
                        for q in range(KC):
                            last = pe.matmul(k.banks[o][:, b * TC:(b + 1) * TC], k.layer[:, b, q, o * P:(o + 1) * P],
                                             chunk_steps(k.A, c)[:, :, q, b], start=(q == 0 and b == 0), stop=(q == KC - 1),
                                             skip_group_check=True)
                    last.then_inc(out_ps, 1)

        @block.vector
        def _(dve):
            dve.sem_inc(out_ready, KC)
            dve.sem_inc(stored[0], 16)
            dve.sem_inc(stored[1], 16)
            with dve.Fori(0, NCH // 2) as i:
                for s in range(2):
                    c = 2 * i + s
                    dve.wait_ge(stored[s], 16 * i + 16)
                    for o in range(KC):
                        dve.wait_ge(out_ps, c * KC + o + 1)
                        dve.scalar_tensor_tensor(o_sb[s][:].rearrange("p (t c b) -> p b t c", c=KC, b=B)[:, :, :, o],
                                                 chunk_steps(k.A, c)[:, :, o, :].rearrange("p t b -> p b t"), 2.0,
                                                 k.banks[o][:, :].rearrange("p (b t) -> p b t", b=B), ALU.mult, ALU.add).then_inc(out_ready, 1)

        @block.sync
        def _(sp):
            with sp.Fori(0, NCH // 2) as i:
                for s in range(2):
                    c = 2 * i + s
                    sp.wait_ge(out_ready, c * KC + 2 * KC)
                    sp.dma_start(out[:, bass.ds(c * (TC * S), TC * S)], o_sb[s][:]).then_inc(stored[s], 16)
            for s in range(2):
                sp.wait_ge(stored[s], 16 * (NCH // 2) + 16)


class Kept:
    pass


def cond_resid_program(nc, dram, out):
    dram["xw"] = nc.dram_tensor("adapter_rows", (B, NPIECE, D), F32, kind="Internal").ap()
    dram["expert_in"] = nc.dram_tensor("expert_in", (E * CAP + NTOK, D), F32, kind="Internal").ap()
    dram["expert_out"] = nc.dram_tensor("expert_out", (E * CAP + 1, D), F32, kind="Internal").ap()
    with ExitStack() as ctx:
        k = Kept()
        keep = lambda n, s, d=F32: ctx.enter_context(nc.sbuf_tensor(n, s, d))
        k.A = keep("acts", [P, (T + 1) * S])
        k.layer = keep("layer", [P, B, KC, D])
        k.vg = keep("gru_const", [P, 3, S])
        k.bgru = keep("gru_bias", [P, 3, KC])
        k.ident = keep("ident", [P, P])
        k.put = keep("put", [P, NT], I32)
        k.get = keep("get", [P, NT], I32)
        k.banks = [ctx.enter_context(nc.psum_tensor(f"bank{n}", [P, 512], F32)) for n in range(8)]
        k.passed = ctx.enter_context(nc.semaphore("passed"))
        k.x_loaded = ctx.enter_context(nc.semaphore("x_loaded"))
        conditioning(nc, k, dram)
        routing(nc, k, dram)
        leaky_recurrence(nc, k, dram)
        experts(nc, k, dram)
        combine(nc, k, dram)
        gru(nc, k, dram)
        adapted_output(nc, k, dram, out)


def kernel(**inputs):
    import numpy as np
    import concourse.bacc as bacc
    from concourse.bass_utils import run_bass_kernel_spmd

    def features_first(a, *axes):
        a = np.ascontiguousarray(a)
        for ax in sorted((x % a.ndim for x in axes), reverse=True):
            s = a.shape
            a = a.reshape(s[:ax] + (4, 4, 32) + s[ax + 1:])
            a = np.moveaxis(a, ax + 1, ax)
            a = a.reshape(s[:ax] + (4, 128) + s[ax + 1:])
        return a

    def moving(w):
        return np.ascontiguousarray(features_first(w, 0).transpose(1, 0, 2))

    def stationary(w):
        return np.ascontiguousarray(features_first(w, 0, 1).transpose(1, 0, 2, 3))

    def vector(v):
        return features_first(v, 0).T

    a = {n: np.asarray(v) for n, v in inputs.items()}
    w0 = a["L0_cond_W"]
    x = features_first(a["x"], 2).transpose(3, 1, 2, 0)
    wk = features_first(a["L1_cond_w_key"], 1).reshape(E, KC, P, FC, P).transpose(0, 2, 1, 3, 4)
    wv = features_first(a["L1_cond_w_value"], 2).reshape(E, FC, P, KC * P).transpose(0, 2, 1, 3)
    w2 = features_first(a["L3_cond_w2"], 0).reshape(KC, P, 2, KC, KC, 32, RANK)
    w2 = w2.transpose(1, 2, 6, 0, 4, 3, 5).reshape(P, NPIECE, KC, D)
    b2 = a["L3_cond_b2"].reshape(2, 4, 4, 32, RANK).transpose(0, 4, 2, 1, 3).reshape(1, NPIECE * D)
    arrays = {
        "x": x.reshape(P, T * S),
        "cond": features_first(a["cond_1024"], 1).transpose(2, 1, 0).reshape(P, S),
        "tok": a["itok_BxS_2_50255"].reshape(NT, P).T,
        "wh": moving(w0[:, :D].T),
        "wz": stationary(w0[:, D:].T),
        "l0v": np.stack([vector(a["L0_cond_b"]), vector(a["L0_cond_alpha"])], 1),
        "maa": np.stack([vector(a["L1_cond_time_maa_k"]), vector(a["L1_cond_time_maa_r"])], 1),
        "w_recept": stationary(a["L1_cond_w_recept"].T),
        "w_key": wk,
        "w_value": wv,
        "ug": np.stack([moving(a["L2_cond_" + n]) for n in ("U_z", "U_r", "U")]),
        "wg": np.stack([stationary(a["L2_cond_" + n]) for n in ("W_z", "W_r", "W")]),
        "cg": np.stack([stationary(a["L2_cond_" + n]) for n in ("C_z", "C_r", "C")]),
        "bgru": np.stack([vector(a["L2_cond_" + n]) for n in ("b_z", "b_r", "b")], 1),
        "base": stationary(a["L3_cond_base_layer"]).reshape(P, KC, D),
        "w1": stationary(a["L3_cond_w1"]),
        "w2": w2,
        "b2": np.broadcast_to(b2, (B, NPIECE * D)),
        "lnb": np.stack([vector(a["L3_cond_" + n]) for n in ("ln_g", "ln_b", "b1")], 1),
    }
    arrays = {f"in_{n}": np.ascontiguousarray(v) for n, v in arrays.items()}
    nc = bacc.Bacc("TRN2", target_bir_lowering=False, num_devices=1)
    dram = {n[3:]: nc.dram_tensor(n, v.shape, mybir.dt.from_np(v.dtype), kind="ExternalInput").ap() for n, v in arrays.items()}
    out = nc.dram_tensor("out", (P, T * S), F32, kind="ExternalOutput").ap()
    cond_resid_program(nc, dram, out)
    got = run_bass_kernel_spmd(nc, [arrays], core_ids=[0]).results[0]["out"]
    return np.ascontiguousarray(np.asarray(got).reshape(4, 32, T, KC, B).transpose(4, 2, 0, 3, 1).reshape(B, T, D))
```

```python
import concourse.bass as bass
from concourse import mybir
from contextlib import ExitStack

F32 = mybir.dt.float32
BF16 = mybir.dt.bfloat16
I32 = mybir.dt.int32
ALU = mybir.AluOpType
ACT = mybir.ActivationFunctionType
AX_X = mybir.AxisListType.X

P = 128
B = 2
T = 2048
D = 512
NG = 4
KC = D // P
S = KC * B
TC = 256
NCH = T // TC
TOKC = TC * B
U = 32
HB = U // 2
NBLK = TC // U
NM = 2
CM = NCH // NM
E = 16
F = 1024
FC = F // P
CAP = B * T // E
SC = CAP // P
NTOK = B * T
NT = NTOK // P
TPC = TOKC // P
TH = TC // P
RANK = 8
LN_EPS = 1e-5
NPIECE = 2 * D * RANK // D
HASH = 5099 % E


def clear_semaphores(nc, sems):
    with nc.Block() as block:
        @block.vector
        def _(dve):
            for sem in sems:
                dve.sem_clear(sem)


def steps8(t, n):
    return t[:, n * S:(n + 1) * S]


def grouped(t):
    return t.rearrange("p (c b) -> p c b", b=B)


def turned(t):
    return t[:, 0:P].rearrange("p (c r) -> p c r", c=KC)[:, :, 0:B]


def wait_alone(k, engine, sem, value):
    engine.wait_ge(sem, value)
    engine.sem_inc(k.passed, 1)


def matvec(pe, bank, w, h):
    for k in range(KC):
        for j in range(NG):
            last = pe.matmul(bank[32 * j:32 * j + B, 0:P], h[:, k, :], w[:, k, j * P:(j + 1) * P],
                             start=(k == 0), stop=(k == KC - 1), tile_position=(0, 32 * j),
                             skip_group_check=True)
    return last


def chunk_steps(a, c):
    return a[:, bass.ds(c * (TC * S) + S, TC * S)].rearrange("p (t c b) -> p t c b", c=KC, b=B)


def minus_previous(dve, dx, k, now, c):
    dve.tensor_tensor(dx[:, 0], k.before[:, bass.ds(c * S, S)].rearrange("p (c b) -> p c b", b=B), now[:, 0], ALU.subtract)
    return dve.tensor_tensor(dx[:, 1:TC], now[:, 0:TC - 1], now[:, 1:TC], ALU.subtract)


def conditioning(nc, k, dram):
    with ExitStack() as ctx:
        sb = lambda n, s, d=F32: ctx.enter_context(nc.sbuf_tensor(n, s, d))
        sem = lambda n: ctx.enter_context(nc.semaphore(n))
        cw = sb("cond_w", [P, 3, KC, KC, P])
        w1 = sb("ada_w1", [P, KC, KC, P])
        w2 = sb("ada_w2", [P, 2, KC, D])
        b2 = sb("ada_b2", [B, 2, D])
        xw = sb("ada_xw", [B, 2, D])
        lnb = sb("ln_gb1", [P, 3, KC])
        low = sb("low_rank", [RANK, 2, B, D])
        base = sb("base", [P, KC, D])
        ones = sb("ones", [P, P])
        cen = sb("centred", [P, S])
        sq = sb("squares", [P, S])
        st = sb("stats", [P, 8])
        ae = sb("ada", [P, S])
        hp = sb("hidden_pre", [P, S])
        hid = sb("hidden", [P, S])
        loads, loads2, low_loaded = sem("c_loads"), sem("c_base"), sem("c_low")
        w2_in = [sem("c_w2_even"), sem("c_w2_odd")]
        xw_ps, xw_ready = sem("c_xw_ps"), sem("c_xw_ready")
        xw_out = [sem("c_xw_out_even"), sem("c_xw_out_odd")]
        v, pes, acts, lowps, lowuse = sem("c_dve"), sem("c_pe"), sem("c_act"), sem("c_lowps"), sem("c_lowuse")
        bank = k.banks
        block = ctx.enter_context(nc.Block())

        @block.sync
        def _(sp):
            sp.dma_start(k.A[:, 0:S], dram["cond"]).then_inc(loads, 16)
            sp.dma_start(lnb[:], dram["lnb"]).then_inc(loads, 16)
            sp.dma_start(k.bgru[:], dram["bgru"]).then_inc(loads, 16)
            sp.dma_start(w1[:], dram["w1"]).then_inc(loads, 16)
            for g in range(3):
                sp.dma_start(cw[:, g], dram["cg"][g]).then_inc(loads, 16)
            with sp.Fori(0, NPIECE // 2) as i:
                for s in range(2):
                    sp.wait_ge(xw_ready, 2 * i + s + 1)
                    sp.dma_start(w2[:, s], dram["w2"][:, bass.ds(2 * i + s, 1)].rearrange("p o k n -> p (o k) n")).then_inc(w2_in[s], 16)
                    sp.dma_start(b2[:, s], dram["b2"][:, bass.ds((2 * i + s) * D, D)]).then_inc(w2_in[s], 16)
            sp.dma_start(base[:], dram["base"]).then_inc(loads2, 16)
            for c in range(NCH):
                sp.dma_start(k.A[:, S + c * TC * S:S + (c + 1) * TC * S],
                             dram["x"][:, c * TC * S:(c + 1) * TC * S]).then_inc(k.x_loaded, 16)
            sp.wait_ge(xw_out[0], 16 * (NPIECE // 2) + 16)
            sp.wait_ge(xw_out[1], 16 * (NPIECE // 2) + 16)
            for h in range(2):
                for b in range(B):
                    sp.dma_start(low[:, h, b, :], dram["xw"][b, h * RANK:(h + 1) * RANK, :]).then_inc(low_loaded, 16)

        @block.vector
        def _(dve):
            n = [0]

            def step(ins):
                n[0] += 1
                ins.then_inc(v, 1)
                dve.wait_ge(v, n[0])

            dve.sem_inc(xw_ready, 2)
            step(dve.memset(ones[:], 1.0))
            dve.wait_ge(loads, 16 * 7)
            dve.wait_ge(pes, 1)
            step(dve.tensor_copy(st[:, 0:2], bank[0][:, 0:2]))
            step(dve.tensor_scalar(st[:, 2:4], st[:, 0:2], 1.0 / D, None, ALU.mult))
            for b in range(B):
                step(dve.tensor_scalar(grouped(cen[:])[:, :, b], grouped(k.A[:, 0:S])[:, :, b], st[:, 2 + b:3 + b], None, ALU.subtract))
            step(dve.tensor_tensor(sq[:], cen[:], cen[:], ALU.mult))
            dve.wait_ge(pes, 2)
            step(dve.tensor_scalar(st[:, 4:6], bank[1][:, 0:2], 1.0 / D, LN_EPS, ALU.mult, ALU.add))
            dve.wait_ge(acts, 1)
            step(dve.reciprocal(st[:, 6:8], st[:, 0:2]))
            for b in range(B):
                step(dve.tensor_scalar(grouped(ae[:])[:, :, b], grouped(cen[:])[:, :, b], st[:, 6 + b:7 + b], None, ALU.mult))
            for b in range(B):
                step(dve.tensor_tensor(grouped(ae[:])[:, :, b], grouped(ae[:])[:, :, b], lnb[:, 0, :], ALU.mult))
            for b in range(B):
                step(dve.tensor_tensor(grouped(ae[:])[:, :, b], grouped(ae[:])[:, :, b], lnb[:, 1, :], ALU.add))
            for g in range(3):
                dve.wait_ge(pes, 3 + g)
                for b in range(B):
                    step(dve.tensor_tensor(grouped(k.vg[:, g])[:, :, b], grouped(bank[2 + g][:, 0:S])[:, :, b], k.bgru[:, g, :], ALU.add))
            dve.wait_ge(pes, 6)
            for b in range(B):
                step(dve.tensor_tensor(grouped(hp[:])[:, :, b], grouped(bank[5][:, 0:S])[:, :, b], lnb[:, 2, :], ALU.add))
            with dve.Fori(0, NPIECE // 2) as i:
                for s in range(2):
                    dve.wait_ge(xw_ps, 2 * i + s + 3)
                    dve.wait_ge(xw_out[s], 16 * i + 16)
                    dve.tensor_tensor(xw[:, s], bank[6 + s][0:B, :], b2[:, s], ALU.add).then_inc(xw_ready, 1)
            dve.wait_ge(loads2, 16)
            for b in range(B):
                for c in range(KC):
                    dve.wait_ge(lowps, b * KC + c + 1)
                    dve.tensor_tensor(k.layer[:, b, c, :], base[:, c, :], bank[(b * KC + c) % 2][:, :], ALU.add).then_inc(lowuse, 1)
            dve.wait_ge(lowuse, B * KC)

        @block.scalar
        def _(act):
            act.wait_ge(v, 7)
            act.activation(st[:, 0:2], st[:, 4:6], ACT.Sqrt).then_inc(acts, 1)
            act.wait_ge(v, 22)
            act.activation(hid[:], hp[:], ACT.Gelu).then_inc(acts, 1)
            act.sem_inc(xw_out[0], 16)
            act.sem_inc(xw_out[1], 16)
            with act.Fori(0, NPIECE // 2) as i:
                for s in range(2):
                    act.wait_ge(xw_ready, 2 * i + s + 3)
                    act.dma_start(dram["xw"][:, bass.ds(2 * i + s, 1), :].rearrange("b o n -> b (o n)"), xw[:, s]).then_inc(xw_out[s], 16)

        @block.tensor
        def _(pe):
            def over_features(out, lhs, rhs):
                for c in range(KC):
                    last = pe.matmul(out, lhs(c), rhs(c), start=(c == 0), stop=(c == KC - 1))
                return last

            pe.sem_inc(xw_ps, 2)
            pe.wait_ge(v, 1)
            pe.wait_ge(loads, 16 * 7)
            cond = grouped(k.A[:, 0:S])
            over_features(bank[0][:, 0:2], lambda c: ones[:], lambda c: cond[:, c, :]).then_inc(pes, 1)
            pe.wait_ge(v, 6)
            over_features(bank[1][:, 0:2], lambda c: ones[:], lambda c: grouped(sq[:])[:, c, :]).then_inc(pes, 1)
            for g in range(3):
                for o in range(KC):
                    last = over_features(bank[2 + g][:, o * B:(o + 1) * B], lambda c: cw[:, g, c, o, :], lambda c: cond[:, c, :])
                last.then_inc(pes, 1)
            pe.wait_ge(v, 14)
            for o in range(KC):
                last = over_features(bank[5][:, o * B:(o + 1) * B], lambda c: w1[:, c, o, :], lambda c: grouped(ae[:])[:, c, :])
            last.then_inc(pes, 1)
            pe.wait_ge(acts, 2)
            with pe.Fori(0, NPIECE // 2) as i:
                for s in range(2):
                    pe.wait_ge(w2_in[s], 32 * i + 32)
                    pe.wait_ge(xw_ready, 2 * i + s + 1)
                    over_features(bank[6 + s][0:B, :], lambda c: grouped(hid[:])[:, c, :], lambda c: w2[:, s, c, :]).then_inc(xw_ps, 1)
            pe.wait_ge(low_loaded, 64)
            for b in range(B):
                for c in range(KC):
                    n = b * KC + c
                    if n >= 2:
                        pe.wait_ge(lowuse, n - 1)
                    pe.matmul(bank[n % 2][:, :], low[:, 0, b, c * P:(c + 1) * P], low[:, 1, b, :], start=True, stop=True).then_inc(lowps, 1)


def routing(nc, k, dram):
    with ExitStack() as ctx:
        sb = lambda n, s, d=F32: ctx.enter_context(nc.sbuf_tensor(n, s, d))
        sem = lambda n: ctx.enter_context(nc.semaphore(n))
        tok = sb("tok", [P, NT], I32)
        ei = sb("expert_i", [P, NT], I32)
        ef = sb("expert", [P, NT])
        iota_e = sb("iota_e", [P, E], I32)
        iota_n = sb("iota_n", [P, NT], I32)
        iota_ef = sb("iota_ef", [P, E])
        trash = sb("trash", [P, NT])
        hot = sb("one_hot", [P, NT, E])
        tot = sb("totals", [P, NT, E])
        run = [sb("run_a", [P, NT, E]), sb("run_b", [P, NT, E])]
        pos = sb("pos", [P, NT])
        keep = sb("keep", [P, NT])
        slot = sb("slot", [P, NT])
        dif = sb("dif", [P, NT])
        upto = sb("upto", [P, P])
        ones = sb("r_ones", [P, P])
        zeros = sb("r_zeros", [P, D])
        tok_in, made, v, counted, zero_out = sem("r_tok"), sem("r_made"), sem("r_dve"), sem("r_counted"), sem("r_zero_out")
        block = ctx.enter_context(nc.Block())

        @block.sync
        def _(sp):
            sp.dma_start(tok[:], dram["tok"]).then_inc(tok_in, 16)
            sp.wait_ge(made, 6)
            for n in range(E * SC):
                sp.dma_start(dram["expert_in"][n * P:(n + 1) * P, :], zeros[:]).then_inc(zero_out, 16)
            sp.dma_start(dram["expert_out"][E * CAP:E * CAP + 1, :], zeros[0:1, :]).then_inc(zero_out, 16)
            sp.wait_ge(zero_out, 16 * (E * SC + 1))

        @block.gpsimd
        def _(pool):
            pool.iota(iota_e[:], pattern=[[1, E]], base=0, channel_multiplier=0).then_inc(made, 1)
            pool.iota(iota_n[:], pattern=[[P, NT]], base=E * CAP, channel_multiplier=1).then_inc(made, 1)
            pool.memset(upto[:], 1.0).then_inc(made, 1)
            pool.memset(k.ident[:], 0.0).then_inc(made, 1)
            pool.memset(ones[:], 1.0).then_inc(made, 1)
            pool.memset(zeros[:], 0.0).then_inc(made, 1)
            pool.wait_ge(made, 6)
            pool.affine_select(out=upto[:], in_=upto[:], pattern=[[1, P]], compare_op=ALU.is_ge, fill=0.0, base=0, channel_multiplier=-1).then_inc(made, 1)
            pool.affine_select(out=k.ident[:], in_=k.ident[:], pattern=[[-1, P]], compare_op=ALU.not_equal, fill=1.0, base=0, channel_multiplier=1).then_inc(made, 1)

        @block.vector
        def _(dve):
            n = [0]

            def step(ins):
                n[0] += 1
                ins.then_inc(v, 1)
                dve.wait_ge(v, n[0])

            dve.wait_ge(tok_in, 16)
            dve.wait_ge(made, 6)
            step(dve.tensor_scalar(ei[:], tok[:], E - 1, None, ALU.bitwise_and))
            step(dve.tensor_scalar(ei[:], ei[:], HASH, None, ALU.mult))
            step(dve.tensor_scalar(ei[:], ei[:], E - 1, None, ALU.bitwise_and))
            step(dve.tensor_copy(ef[:], ei[:]))
            step(dve.tensor_copy(iota_ef[:], iota_e[:]))
            step(dve.tensor_copy(trash[:], iota_n[:]))
            step(dve.tensor_tensor(hot[:], ef[:].unsqueeze(2).to_broadcast([P, NT, E]), iota_ef[:].unsqueeze(1).to_broadcast([P, NT, E]), ALU.is_equal))
            dve.wait_ge(counted, 1)
            step(dve.tensor_copy(tot[:].rearrange("p n e -> p (n e)"), k.banks[1][:, :]))
            step(dve.tensor_copy(run[0][:], tot[:]))
            a = 0
            d = 1
            while d < NT:
                step(dve.tensor_copy(run[1 - a][:, 0:d], run[a][:, 0:d]))
                step(dve.tensor_tensor(run[1 - a][:, d:NT], run[a][:, d:NT], run[a][:, 0:NT - d], ALU.add))
                a = 1 - a
                d *= 2
            step(dve.tensor_tensor(tot[:], run[a][:], tot[:], ALU.subtract))
            step(dve.tensor_tensor(tot[:], tot[:], k.banks[0][:, :].rearrange("p (n e) -> p n e", e=E), ALU.add))
            step(dve.tensor_tensor(tot[:], tot[:], hot[:], ALU.mult))
            step(dve.tensor_reduce(pos[:], tot[:], AX_X, ALU.add))
            step(dve.tensor_scalar(keep[:], pos[:], float(CAP), None, ALU.is_le))
            step(dve.tensor_scalar(slot[:], ef[:], float(CAP), -1.0, ALU.mult, ALU.add))
            step(dve.tensor_tensor(slot[:], slot[:], pos[:], ALU.add))
            step(dve.tensor_tensor(dif[:], slot[:], trash[:], ALU.subtract))
            step(dve.tensor_tensor(dif[:], dif[:], keep[:], ALU.mult))
            step(dve.tensor_tensor(dif[:], dif[:], trash[:], ALU.add))
            step(dve.tensor_copy(k.put[:], dif[:]))
            step(dve.tensor_scalar(slot[:], slot[:], -float(E * CAP), None, ALU.add))
            step(dve.tensor_tensor(slot[:], slot[:], keep[:], ALU.mult))
            step(dve.tensor_scalar(slot[:], slot[:], float(E * CAP), None, ALU.add))
            step(dve.tensor_copy(k.get[:], slot[:]))

        @block.tensor
        def _(pe):
            pe.wait_ge(made, 8)
            pe.wait_ge(v, 7)
            flat = hot[:].rearrange("p n e -> p (n e)")
            pe.matmul(k.banks[0][:, :], upto[:], flat, start=True, stop=True)
            pe.matmul(k.banks[1][:, :], ones[:], flat, start=True, stop=True).then_inc(counted, 1)


def recurrences(nc, k, dram, leaky, gru):
    Z, R, H = range(3)
    with_l, with_g = leaky is not None, gru is not None
    tag = k.next_run()
    with ExitStack() as ctx:
        sb = lambda n, s, d=F32: ctx.enter_context(nc.sbuf_tensor(n + tag, s, d))
        sems = []

        def sem(n):
            sems.append(ctx.enter_context(nc.semaphore(n + tag)))
            return sems[-1]

        loads, ready = sem("s_loads"), sem("s_ready")
        if with_l:
            wh = sb("l_wh", [P, KC, D])
            wz = sb("l_wz", [P, KC, KC, P])
            vecs = sb("l_b_alpha", [P, 2, KC])
            leak = sb("leak", [P, S])
            xz = sb("l_xz", [P, TC * S])
            xz_ring = sb("l_xz_ring", [P, U * S])
            x_ring = sb("l_x_ring", [P, U * S])
            warm = sb("warm", [P, D], BF16)
            tl = sb("l_t", [P, P])
            pl, gl, gx, hl, up = (sb(n, [P, S]) for n in ("l_pre", "l_gate", "l_gate_x", "l_h_leak", "l_update"))
            l_proj, l_projected, l_staged, l_ps, l_pre, l_gate, l_chain, l_h, l_added = (sem("l_" + n) for n in (
                "proj", "projected", "staged", "ps", "pre", "gate", "chain", "h", "added"))
            bl = k.banks[7]
        if with_g:
            ug = sb("g_u", [P, 3, KC, D])
            wg = sb("g_w", [P, 3, KC, KC, P])
            xg = sb("g_x", [P, 3, TC * S])
            g_ring = sb("g_ring", [P, 3, U * S])
            tz, tr, th = (sb(n, [P, P]) for n in ("z_t", "r_t", "h_t"))
            pz, pr, ph, gz, gr, gh, rh, zh, keep = (sb(n, [P, S]) for n in (
                "pre_z", "pre_r", "pre_h", "gate_z", "gate_r", "cand", "rh", "z_cand", "keep_h"))
            g_proj, g_projected, g_staged, g_added = (sem("g_" + n) for n in ("proj", "projected", "staged", "added"))
            r_ps, z_ps, h_ps, pre_r, pre_z, pre_h, r_gate, z_gate, cand, rh_ready, g_chain, g_h = (sem("g_" + n) for n in (
                "r_ps", "z_ps", "h_ps", "pre_r", "pre_z", "pre_h", "r_gate", "z_gate", "cand", "rh_ready", "chain", "h"))
            bz, br, bh = k.banks[4], k.banks[5], k.banks[6]
        n_loads = 16 * (3 * with_l + 6 * with_g)
        block = ctx.enter_context(nc.Block())

        @block.sync
        def _(sp):
            if with_l:
                sp.dma_start(wh[:], dram["wh"]).then_inc(loads, 16)
                sp.dma_start(wz[:], dram["wz"]).then_inc(loads, 16)
                sp.dma_start(vecs[:], dram["l0v"]).then_inc(loads, 16)
            if with_g:
                for g in range(3):
                    sp.dma_start(ug[:, g], dram["ug"][g]).then_inc(loads, 16)
                    sp.dma_start(wg[:, g], dram["wg"][g]).then_inc(loads, 16)

        @block.tensor
        def _(pe):
            pe.wait_ge(loads, n_loads)
            pe.wait_ge(ready, 1)
            with pe.Fori(0, CM) as c:
                if with_l:
                    for o in range(KC):
                        if with_g:
                            pe.wait_ge(g_projected, c * (3 * KC) + KC)
                        for q in range(KC):
                            last = pe.matmul(k.banks[o][:, :], wz[:, q, o, :], chunk_steps(k.A, leaky * CM + c)[:, :, q, :],
                                             start=(q == 0), stop=(q == KC - 1))
                        last.then_inc(l_proj, 1)
                if with_g:
                    for g in range(3):
                        for o in range(KC):
                            if with_l and g == 0:
                                pe.wait_ge(l_projected, c * KC + o + 1)
                            pe.wait_ge(g_projected, c * (3 * KC) + g * KC + o + 1)
                            for q in range(KC):
                                last = pe.matmul(k.banks[o][:, :], wg[:, g, q, o, :], chunk_steps(k.A, gru * CM + c)[:, :, q, :],
                                                 start=(q == 0), stop=(q == KC - 1))
                            last.then_inc(g_proj, 1)
                with pe.Fori(0, NBLK) as i:
                    for u in range(U):
                        st = c * TC + i * U + u
                        if with_l:
                            pe.wait_ge(l_h, st + 1)
                            matvec(pe, bl, wh, grouped(steps8(k.h_leaky, (u - 1) % U))).then_inc(l_ps, 1)
                        if with_g:
                            h = grouped(steps8(k.h_gru, (u - 1) % U))
                            pe.wait_ge(g_h, st + 1)
                            matvec(pe, br, ug[:, R], h).then_inc(r_ps, 1)
                            matvec(pe, bz, ug[:, Z], h).then_inc(z_ps, 1)
                            pe.wait_ge(rh_ready, st + 1)
                            matvec(pe, bh, ug[:, H], grouped(rh[:])).then_inc(h_ps, 1)
                        else:
                            for _ in range(3):
                                pe.matmul(k.banks[5][0:B, :], warm[:, 0:B], warm[:, :], start=True, stop=True)

        @block.scalar
        def _(act):
            act.wait_ge(loads, n_loads)
            act.wait_ge(ready, 1)
            if with_g:
                act.sem_inc(g_projected, KC)
            with act.Fori(0, CM) as c:
                if with_l:
                    act.wait_ge(l_added, c * (2 * NBLK) + 2)
                    for o in range(KC):
                        act.wait_ge(l_proj, c * KC + o + 1)
                        act.activation(xz[:].rearrange("p (t c b) -> p t c b", c=KC, b=B)[:, :, o, :],
                                       k.banks[o][:, :].rearrange("p (t b) -> p t b", b=B),
                                       ACT.Identity, bias=vecs[:, 0, o:o + 1]).then_inc(l_projected, 1)
                if with_g:
                    act.wait_ge(g_added, c * (2 * NBLK) + 2)
                    for g in range(3):
                        for o in range(KC):
                            act.wait_ge(g_proj, c * (3 * KC) + g * KC + o + 1)
                            for b in range(B):
                                last = act.activation(xg[:, g].rearrange("p (t c b) -> p t c b", c=KC, b=B)[:, :, o, b],
                                                      k.banks[o][:, :].rearrange("p (t b) -> p t b", b=B)[:, :, b],
                                                      ACT.Identity, bias=k.vg[:, g, o * B + b:o * B + b + 1])
                            last.then_inc(g_projected, 1)
                with act.Fori(0, NBLK) as i:
                    for u in range(U):
                        st = c * TC + i * U + u
                        if with_l:
                            act.wait_ge(l_pre, st + 1)
                            act.activation(gl[:], pl[:], ACT.Sigmoid).then_inc(l_gate, 1)
                        if with_g:
                            act.wait_ge(pre_r, st + 1)
                            act.activation(gr[:], pr[:], ACT.Sigmoid).then_inc(r_gate, 1)
                        if with_l:
                            act.wait_ge(l_chain, 4 * st + 4)
                            if u % HB == 0:
                                act.wait_ge(l_added, (c * NBLK + i) * 2 + u // HB + 1)
                            act.activation(steps8(k.h_leaky, u), up[:], ACT.Tanh).then_inc(l_h, 1)
                        if with_g:
                            act.wait_ge(pre_z, st + 1)
                            act.activation(gz[:], pz[:], ACT.Sigmoid).then_inc(z_gate, 1)
                            act.wait_ge(pre_h, st + 1)
                            act.activation(gh[:], ph[:], ACT.Tanh).then_inc(cand, 1)

        @block.gpsimd
        def _(pool):
            def halves():
                for half in range(2):
                    yield half, half * HB * S, (half + 1) * HB * S

            def span_steps(span, c, at):
                return k.A[:, bass.ds(S + (span * CM + c) * (TC * S) + at, HB * S)]

            def add_half(c, i, half, a, b):
                through = c * TC + i * U + (half + 1) * HB + 1
                for on, span, h, ring, added in recurring:
                    if on:
                        pool.wait_ge(h, through)
                        here = span_steps(span, c, i * (U * S) + a)
                        pool.tensor_tensor(here, here, ring[:, a:b], ALU.add).then_inc(added, 1)

            recurring = [(with_l, leaky, l_h if with_l else None, k.h_leaky, l_added if with_l else None),
                         (with_g, gru, g_h if with_g else None, k.h_gru, g_added if with_g else None)]
            if with_l:
                pool.sem_inc(l_added, 2)
            if with_g:
                pool.sem_inc(g_added, 2)
            with pool.Fori(0, CM) as c:
                for half, a, b in halves():
                    if with_l:
                        if half == 0:
                            wait_alone(k, pool, l_projected, (c + 1) * KC)
                        pool.tensor_copy(xz_ring[:, a:b], xz[:, a:b]).then_inc(l_staged, 1)
                        pool.tensor_copy(x_ring[:, a:b], span_steps(leaky, c, a)).then_inc(l_staged, 1)
                    if with_g:
                        if half == 0:
                            wait_alone(k, pool, g_projected, (c + 1) * (3 * KC) + KC)
                        pool.tensor_copy(g_ring[:, :, a:b], xg[:, :, a:b]).then_inc(g_staged, 1)
                with pool.Fori(0, NBLK - 1) as i:
                    for half, a, b in halves():
                        add_half(c, i, half, a, b)
                        ahead = (i + 1) * (U * S) + a
                        if with_l:
                            pool.tensor_copy(xz_ring[:, a:b], xz[:, bass.ds(ahead, HB * S)]).then_inc(l_staged, 1)
                            pool.tensor_copy(x_ring[:, a:b], span_steps(leaky, c, ahead)).then_inc(l_staged, 1)
                        if with_g:
                            pool.tensor_copy(g_ring[:, :, a:b], xg[:, :, bass.ds(ahead, HB * S)]).then_inc(g_staged, 1)
                for half, a, b in halves():
                    add_half(c, NBLK - 1, half, a, b)

        @block.vector
        def _(dve):
            if with_l:
                dve.wait_ge(loads, n_loads)
                for b in range(B):
                    dve.tensor_scalar(grouped(leak[:])[:, :, b], vecs[:, 1, :], -1.0, 1.0, ALU.mult, ALU.add)
                dve.memset(warm[:], 0.0)
                dve.memset(bl[:, 0:P], 0.0)
                dve.sem_inc(l_h, 1)
            if with_g:
                for t in (bz, br, bh):
                    dve.memset(t[:, 0:P], 0.0)
                dve.sem_inc(g_h, 1)
            if with_l and isinstance(leaky, int) and leaky == 0:
                dve.memset(steps8(k.h_gru, U - 1), 0.0)
                dve.tensor_copy(k.before[:, 0:S], k.A[:, 0:S])
                dve.tensor_copy(steps8(k.h_leaky, U - 1), k.A[:, 0:S]).then_inc(ready, 1)
            else:
                dve.memset(rh[:], 0.0).then_inc(ready, 1)
            dve.wait_ge(ready, 1)

            def pre_activation(bank, t, x, out, ps, st, chain, links, done):
                dve.wait_ge(ps, st + 1)
                dve.transpose(t[:], bank[:, 0:P]).then_inc(chain, 1)
                dve.wait_ge(chain, links)
                dve.tensor_tensor(grouped(out[:]), turned(t), grouped(x), ALU.add).then_inc(done, 1)

            with dve.Fori(0, CM) as c:
                with dve.Fori(0, NBLK) as i:
                    for u in range(U):
                        st = c * TC + i * U + u
                        if with_l:
                            if u % HB == 0:
                                dve.wait_ge(l_staged, (c * NBLK + i) * 4 + 2 * (u // HB) + 2)
                            dve.wait_ge(l_h, st + 1)
                            dve.tensor_tensor(hl[:], steps8(k.h_leaky, (u - 1) % U), leak[:], ALU.mult).then_inc(l_chain, 1)
                            pre_activation(bl, tl, steps8(xz_ring, u), pl, l_ps, st, l_chain, 4 * st + 2, l_pre)
                        if with_g:
                            if u % HB == 0:
                                dve.wait_ge(g_staged, (c * NBLK + i) * 2 + (u // HB) + 1)
                            h = steps8(k.h_gru, (u - 1) % U)
                            pre_activation(br, tr, steps8(g_ring[:, R], u), pr, r_ps, st, g_chain, 5 * st + 1, pre_r)
                        if with_l:
                            dve.wait_ge(l_gate, st + 1)
                            dve.tensor_tensor(gx[:], gl[:], steps8(x_ring, u), ALU.mult).then_inc(l_chain, 1)
                            dve.wait_ge(l_chain, 4 * st + 3)
                            dve.tensor_tensor(up[:], gx[:], hl[:], ALU.add).then_inc(l_chain, 1)
                        if with_g:
                            dve.wait_ge(r_gate, st + 1)
                            dve.tensor_tensor(rh[:], gr[:], h, ALU.mult).then_inc(rh_ready, 1)
                            pre_activation(bz, tz, steps8(g_ring[:, Z], u), pz, z_ps, st, g_chain, 5 * st + 2, pre_z)
                            dve.wait_ge(z_gate, st + 1)
                            dve.scalar_tensor_tensor(keep[:], gz[:], -1.0, h, ALU.add, ALU.mult).then_inc(g_chain, 1)
                            pre_activation(bh, th, steps8(g_ring[:, H], u), ph, h_ps, st, g_chain, 5 * st + 4, pre_h)
                            dve.wait_ge(cand, st + 1)
                            dve.tensor_tensor(zh[:], gz[:], gh[:], ALU.mult).then_inc(g_chain, 1)
                            dve.wait_ge(g_chain, 5 * st + 5)
                            if u % HB == 0:
                                dve.wait_ge(g_added, (c * NBLK + i) * 2 + u // HB + 1)
                            dve.tensor_tensor(steps8(k.h_gru, u), zh[:], keep[:], ALU.subtract).then_inc(g_h, 1)
    clear_semaphores(nc, sems)


def experts(nc, k, dram, m):
    tag = k.next_run()
    with ExitStack() as ctx:
        sb = lambda n, s, d=F32: ctx.enter_context(nc.sbuf_tensor(n + tag, s, d))
        sems = []

        def sem(n):
            sems.append(ctx.enter_context(nc.semaphore(n + tag)))
            return sems[-1]

        maa = sb("maa", [P, 2, KC])
        key = [sb(f"w_key{s}", [P, KC, FC, P]) for s in range(2)]
        val = [sb(f"w_value{s}", [P, FC, D]) for s in range(2)]
        w_in = [sem(f"m_w_in{s}") for s in range(2)]
        maa_in, shifted, mixed, rows_t, rows_ready, idx_ready, scattered, rows_free = (sem("m_" + n) for n in (
            "maa_in", "shifted", "mixed", "rows_t", "rows_ready", "idx_ready", "scattered", "rows_free"))
        with ExitStack() as c1:
            dx = c1.enter_context(nc.sbuf_tensor("dx" + tag, [P, TC, KC, B], F32))
            xk = c1.enter_context(nc.sbuf_tensor("xk" + tag, [P, KC, B, TC], F32))
            rows = c1.enter_context(nc.sbuf_tensor("rows" + tag, [P, TPC, D], F32))
            put = [c1.enter_context(nc.sbuf_tensor(f"put{n}" + tag, [P, 1], I32)) for n in range(TPC)]
            block = c1.enter_context(nc.Block())

            @block.sync
            def _(sp):
                sp.dma_start(maa[:], dram["maa"]).then_inc(maa_in, 16)
                for s in range(2):
                    sp.dma_start(key[s][:], dram["w_key"][s]).then_inc(w_in[s], 16)
                    sp.dma_start(val[s][:], dram["w_value"][s]).then_inc(w_in[s], 16)

            @block.vector
            def _(dve):
                dve.wait_ge(maa_in, 16)
                dve.sem_inc(mixed, 1)
                with dve.Fori(0, CM) as c:
                    now = chunk_steps(k.A, m * CM + c)
                    dve.tensor_copy(k.before[:, bass.ds((m * CM + c + 1) * S, S)], k.A[:, bass.ds((m * CM + c + 1) * (TC * S), S)]).then_inc(shifted, 1)
                    minus_previous(dve, dx, k, now, m * CM + c).then_inc(shifted, 1)
                    dve.wait_ge(shifted, 2 * c + 2)
                    dve.wait_ge(rows_t, c * TPC + TPC)
                    for o in range(KC):
                        last = dve.scalar_tensor_tensor(xk[:, o].rearrange("p b t -> p t b"), dx[:, :, o, :], maa[:, 0, o:o + 1],
                                                 now[:, :, o, :], ALU.mult, ALU.add)
                    last.then_inc(mixed, 1)
                    dve.wait_ge(mixed, c + 2)
                    wait_alone(k, dve, rows_free, c + 1)
                    for n in range(TPC):
                        last = dve.tensor_copy(put[n][:], k.put[:, bass.ds((m * CM + c) * TH + (n // TH) * (NT // B) + n % TH, 1)])
                    last.then_inc(idx_ready, 1)

            @block.tensor
            def _(pe):
                pe.sem_inc(rows_t, TPC)
                with pe.Fori(0, CM) as c:
                    pe.wait_ge(mixed, c + 2)
                    for n in range(TPC):
                        pe.wait_ge(rows_ready, c * TPC + n + 1)
                        for o in range(KC):
                            last = pe.transpose(k.banks[n][:, o * P:(o + 1) * P], xk[:, o, n // TH, (n % TH) * P:(n % TH + 1) * P], k.ident[:])
                        last.then_inc(rows_t, 1)

            @block.scalar
            def _(act):
                act.sem_inc(rows_ready, TPC)
                with act.Fori(0, CM) as c:
                    act.wait_ge(rows_free, c + 1)
                    for n in range(TPC):
                        act.wait_ge(rows_t, c * TPC + n + 1 + TPC)
                        act.activation(rows[:, n, :], k.banks[n][:, :], ACT.Copy).then_inc(rows_ready, 1)

            @block.gpsimd
            def _(pool):
                pool.sem_inc(rows_free, 1)
                with pool.Fori(0, CM) as c:
                    pool.wait_ge(idx_ready, c + 1)
                    for n in range(TPC):
                        wait_alone(k, pool, rows_ready, c * TPC + n + 1 + TPC)
                        pool.indirect_dma_start(out=dram["expert_in"][:, :], out_offset=bass.IndirectOffsetOnAxis(ap=put[n][:, 0:1], axis=0),
                                                in_=rows[:, n, :], in_offset=None).then_inc(scattered, 16)
                    pool.wait_ge(scattered, 16 * TPC * (c + 1))
                    pool.sem_inc(rows_free, 1)

        with ExitStack() as c2:
            xin = [c2.enter_context(nc.sbuf_tensor(f"xin{s}" + tag, [P, SC, D], F32)) for s in range(2)]
            xt = c2.enter_context(nc.sbuf_tensor("xt" + tag, [P, KC, CAP], F32))
            rel = [c2.enter_context(nc.sbuf_tensor(f"relu{s}" + tag, [P, CAP], F32)) for s in range(2)]
            hid = c2.enter_context(nc.sbuf_tensor("hid" + tag, [P, FC, CAP], F32))
            yo = c2.enter_context(nc.sbuf_tensor("yo" + tag, [P, SC, D], F32))
            x_in = [sem(f"m_x_in{s}") for s in range(2)]
            turned_ps, xt_ready, key_ps, rel_ready, hid_ready, val_ps, yo_ready, y_out = (
                sem("m_" + n) for n in (
                    "turned_ps", "xt_ready", "key_ps", "rel_ready", "hid_ready", "val_ps", "yo_ready", "y_out"))
            block = c2.enter_context(nc.Block())

            @block.sync
            def _(sp):
                for s in range(2):
                    sp.dma_start(xin[s][:], dram["expert_in"][s * CAP:(s + 1) * CAP, :].rearrange("(s p) d -> p s d", p=P)).then_inc(x_in[s], 16)
                with sp.Fori(0, E // 2 - 1) as i:
                    for s in range(2):
                        sp.wait_ge(val_ps, (2 * i + s + 2) * SC)
                        nxt = 2 * i + s + 2
                        sp.dma_start(key[s][:], dram["w_key"][bass.ds(nxt, 1)].rearrange("e p a b c -> (e p) a b c")).then_inc(w_in[s], 16)
                        sp.dma_start(val[s][:], dram["w_value"][bass.ds(nxt, 1)].rearrange("e p a b -> (e p) a b")).then_inc(w_in[s], 16)
                        sp.dma_start(xin[s][:], dram["expert_in"][bass.ds(nxt * CAP, CAP), :].rearrange("(s p) d -> p s d", p=P)).then_inc(x_in[s], 16)

            @block.tensor
            def _(pe):
                pe.sem_inc(key_ps, FC)
                pe.sem_inc(val_ps, SC)
                with pe.Fori(0, E // 2) as i:
                    for s in range(2):
                        e = 2 * i + s
                        pe.wait_ge(x_in[s], 16 * i + 16)
                        pe.wait_ge(xt_ready, e * SC + SC)
                        for h in range(SC):
                            for o in range(KC):
                                last = pe.transpose(k.banks[h][:, o * P:(o + 1) * P], xin[s][:, h, o * P:(o + 1) * P], k.ident[:])
                            last.then_inc(turned_ps, 1)
                        pe.wait_ge(w_in[s], 32 * i + 32)
                        pe.wait_ge(xt_ready, e * SC + 2 * SC)
                        for f in range(FC):
                            pe.wait_ge(rel_ready, e * FC + f + 1)
                            for o in range(KC):
                                last = pe.matmul(k.banks[2 + f % 2][:, 0:CAP], key[s][:, o, f, :], xt[:, o, :], start=(o == 0), stop=(o == KC - 1))
                            last.then_inc(key_ps, 1)
                        pe.wait_ge(hid_ready, e * FC + FC + 2)
                        pe.wait_ge(yo_ready, e * SC + SC)
                        for h in range(SC):
                            for f in range(FC):
                                last = pe.matmul(k.banks[4 + h][:, :], hid[:, f, h * P:(h + 1) * P], val[s][:, f, :], start=(f == 0), stop=(f == FC - 1))
                            last.then_inc(val_ps, 1)

            @block.scalar
            def _(act):
                act.sem_inc(rel_ready, 2)
                with act.Fori(0, E) as e:
                    for f in range(FC):
                        act.wait_ge(key_ps, e * FC + f + 1 + FC)
                        act.wait_ge(hid_ready, e * FC + f + 1)
                        act.activation(rel[f % 2][:], k.banks[2 + f % 2][:, 0:CAP], ACT.Relu).then_inc(rel_ready, 1)
                    act.wait_ge(yo_ready, e * SC + 2 * SC)
                    act.dma_start(dram["expert_out"][bass.ds(e * CAP, CAP), :].rearrange("(s p) d -> p s d", p=P), yo[:]).then_inc(y_out, 16)
                act.wait_ge(y_out, 16 * (E + 1))

            @block.vector
            def _(dve):
                dve.sem_inc(xt_ready, SC)
                dve.sem_inc(hid_ready, 2)
                dve.sem_inc(yo_ready, SC)
                dve.sem_inc(y_out, 16)
                with dve.Fori(0, E) as e:
                    dve.wait_ge(key_ps, e * FC + FC)
                    for h in range(SC):
                        dve.wait_ge(turned_ps, e * SC + h + 1)
                        dve.tensor_copy(xt[:, :, h * P:(h + 1) * P], k.banks[h][:, :].rearrange("p (c t) -> p c t", c=KC)).then_inc(xt_ready, 1)
                    dve.wait_ge(val_ps, e * SC + SC)
                    for f in range(FC):
                        dve.wait_ge(rel_ready, e * FC + f + 1 + 2)
                        dve.tensor_tensor(hid[:, f, :], rel[f % 2][:], rel[f % 2][:], ALU.mult).then_inc(hid_ready, 1)
                    dve.wait_ge(y_out, 16 * e + 16)
                    for h in range(SC):
                        dve.wait_ge(val_ps, e * SC + h + 1 + SC)
                        dve.tensor_copy(yo[:, h, :], k.banks[4 + h][:, :]).then_inc(yo_ready, 1)
    clear_semaphores(nc, sems)


def combine(nc, k, dram, m):
    tag = k.next_run()
    with ExitStack() as ctx:
        sb = lambda n, s, d=F32: ctx.enter_context(nc.sbuf_tensor(n + tag, s, d))
        sems = []

        def sem(n):
            sems.append(ctx.enter_context(nc.semaphore(n + tag)))
            return sems[-1]

        maa = sb("maa_again", [P, 2, KC])
        wr = sb("w_recept", [P, KC, KC, P])
        dx = sb("dxr", [P, TC, KC, B])
        xr = sb("xr", [P, KC, TOKC])
        r = sb("recept", [P, KC, TC, B])
        get = [sb(f"get{n}", [P, 1], I32) for n in range(TPC)]
        y = sb("y_rows", [P, TPC, D])
        ry = sb("r_times_y", [P, TPC, KC, P])
        loads, shifted, mixed, r_ps, r_ready, idx_ready, yt_ps, mulled, added = (sem("g_" + n) for n in (
            "loads", "shifted", "mixed", "r_ps", "r_ready", "idx_ready", "yt_ps", "mulled", "added"))
        gathered = [sem(f"g_gathered{n}") for n in range(TPC)]
        block = ctx.enter_context(nc.Block())

        @block.sync
        def _(sp):
            sp.dma_start(maa[:], dram["maa"]).then_inc(loads, 16)
            sp.dma_start(wr[:], dram["w_recept"]).then_inc(loads, 16)

        @block.vector
        def _(dve):
            dve.wait_ge(loads, 32)
            dve.sem_inc(mulled, TPC)
            with dve.Fori(0, CM) as i:
                now = chunk_steps(k.A, m * CM + i)
                wait_alone(k, dve, yt_ps, i * TPC + TPC)
                for n in range(TPC):
                    last = dve.tensor_copy(get[n][:], k.get[:, bass.ds((m * CM + i) * TH + (n // TH) * (NT // B) + n % TH, 1)])
                last.then_inc(idx_ready, 1)
                minus_previous(dve, dx, k, now, m * CM + i).then_inc(shifted, 1)
                dve.wait_ge(shifted, i + 1)
                dve.wait_ge(r_ps, i * KC + KC)
                for o in range(KC):
                    last = dve.scalar_tensor_tensor(xr[:, o].rearrange("p (t b) -> p t b", b=B), dx[:, :, o, :], maa[:, 1, o:o + 1],
                                                    now[:, :, o, :], ALU.mult, ALU.add)
                last.then_inc(mixed, 1)
                dve.wait_ge(r_ready, i * KC + 2 * KC)
                for n in range(TPC):
                    b, h = n // TH, n % TH
                    dve.wait_ge(yt_ps, i * TPC + n + 1 + TPC)
                    dve.tensor_tensor(ry[:, n], r[:, :, h * P:(h + 1) * P, b], k.banks[4 + n][:, :].rearrange("p (c t) -> p c t", c=KC), ALU.mult).then_inc(mulled, 1)
                    dve.wait_ge(mulled, i * TPC + n + 1 + TPC)
                    here = k.A[:, bass.ds(S + (m * CM + i) * (TC * S) + h * (P * S), P * S)].rearrange("p (t c b) -> p c t b", c=KC, b=B)[:, :, :, b]
                    dve.tensor_tensor(here, here, ry[:, n], ALU.add).then_inc(added, 1)
                dve.wait_ge(added, (i + 1) * TPC)

        @block.tensor
        def _(pe):
            pe.wait_ge(loads, 32)
            pe.sem_inc(yt_ps, TPC)
            pe.sem_inc(r_ps, KC)
            with pe.Fori(0, CM) as i:
                pe.wait_ge(mixed, i + 1)
                pe.wait_ge(r_ready, i * KC + KC)
                for o in range(KC):
                    for q in range(KC):
                        last = pe.matmul(k.banks[o][:, :], wr[:, q, o, :], xr[:, q, :], start=(q == 0), stop=(q == KC - 1))
                    last.then_inc(r_ps, 1)
                for n in range(TPC):
                    pe.wait_ge(gathered[n], 16 * i + 16)
                    pe.wait_ge(mulled, i * TPC + n + 1)
                    for o in range(KC):
                        last = pe.transpose(k.banks[4 + n][:, o * P:(o + 1) * P], y[:, n, o * P:(o + 1) * P], k.ident[:])
                    last.then_inc(yt_ps, 1)

        @block.scalar
        def _(act):
            act.sem_inc(r_ready, KC)
            with act.Fori(0, CM) as i:
                act.wait_ge(mulled, i * TPC + TPC)
                for o in range(KC):
                    act.wait_ge(r_ps, i * KC + o + 1 + KC)
                    act.activation(r[:, o].rearrange("p t b -> p (t b)"), k.banks[o][:, :], ACT.Sigmoid).then_inc(r_ready, 1)

        @block.gpsimd
        def _(pool):
            with pool.Fori(0, CM) as i:
                pool.wait_ge(idx_ready, i + 1)
                wait_alone(k, pool, yt_ps, i * TPC + TPC)
                for n in range(TPC):
                    pool.indirect_dma_start(out=y[:, n, :], out_offset=None, in_=dram["expert_out"][:, :],
                                            in_offset=bass.IndirectOffsetOnAxis(ap=get[n][:, 0:1], axis=0)).then_inc(gathered[n], 16)
    clear_semaphores(nc, sems)


def adapted_output(nc, k, dram, out):
    with ExitStack() as ctx:
        sem = lambda n: ctx.enter_context(nc.semaphore(n))
        o_sb = [ctx.enter_context(nc.sbuf_tensor(f"out_sb{s}", [P, TC * S], F32)) for s in range(2)]
        out_ps, out_ready = sem("o_ps"), sem("o_ready")
        stored = [sem("o_stored0"), sem("o_stored1")]
        block = ctx.enter_context(nc.Block())

        @block.tensor
        def _(pe):
            with pe.Fori(0, NCH) as c:
                for o in range(KC):
                    pe.wait_ge(out_ready, c * KC + o + 1)
                    for b in range(B):
                        for q in range(KC):
                            last = pe.matmul(k.banks[o][:, b * TC:(b + 1) * TC], k.layer[:, b, q, o * P:(o + 1) * P],
                                             chunk_steps(k.A, c)[:, :, q, b], start=(q == 0 and b == 0), stop=(q == KC - 1),
                                             skip_group_check=True)
                    last.then_inc(out_ps, 1)

        @block.vector
        def _(dve):
            dve.sem_inc(out_ready, KC)
            dve.sem_inc(stored[0], 16)
            dve.sem_inc(stored[1], 16)
            with dve.Fori(0, NCH // 2) as i:
                for s in range(2):
                    c = 2 * i + s
                    dve.wait_ge(stored[s], 16 * i + 16)
                    for o in range(KC):
                        dve.wait_ge(out_ps, c * KC + o + 1)
                        dve.scalar_tensor_tensor(o_sb[s][:].rearrange("p (t c b) -> p b t c", c=KC, b=B)[:, :, :, o],
                                                 chunk_steps(k.A, c)[:, :, o, :].rearrange("p t b -> p b t"), 2.0,
                                                 k.banks[o][:, :].rearrange("p (b t) -> p b t", b=B), ALU.mult, ALU.add).then_inc(out_ready, 1)

        @block.sync
        def _(sp):
            with sp.Fori(0, NCH // 2) as i:
                for s in range(2):
                    c = 2 * i + s
                    sp.wait_ge(out_ready, c * KC + 2 * KC)
                    sp.dma_start(out[:, bass.ds(c * (TC * S), TC * S)], o_sb[s][:]).then_inc(stored[s], 16)
            for s in range(2):
                sp.wait_ge(stored[s], 16 * (NCH // 2) + 16)


class Kept:
    runs = 0

    def next_run(self):
        self.runs += 1
        return f"_run{self.runs}"


def cond_resid_program(nc, dram, out):
    dram["xw"] = nc.dram_tensor("adapter_rows", (B, NPIECE, D), F32, kind="Internal").ap()
    dram["expert_in"] = nc.dram_tensor("expert_in", (E * CAP + NTOK, D), F32, kind="Internal").ap()
    dram["expert_out"] = nc.dram_tensor("expert_out", (E * CAP + 1, D), F32, kind="Internal").ap()
    with ExitStack() as ctx:
        k = Kept()
        keep = lambda n, s, d=F32: ctx.enter_context(nc.sbuf_tensor(n, s, d))
        k.A = keep("acts", [P, (T + 1) * S])
        k.layer = keep("layer", [P, B, KC, D])
        k.vg = keep("gru_const", [P, 3, S])
        k.bgru = keep("gru_bias", [P, 3, KC])
        k.ident = keep("ident", [P, P])
        k.h_leaky = keep("h_leaky", [P, U * S])
        k.h_gru = keep("h_gru", [P, U * S])
        k.before = keep("before", [P, (NCH + 1) * S])
        k.put = keep("put", [P, NT], I32)
        k.get = keep("get", [P, NT], I32)
        k.banks = [ctx.enter_context(nc.psum_tensor(f"bank{n}", [P, 512], F32)) for n in range(8)]
        k.passed = ctx.enter_context(nc.semaphore("passed"))
        k.x_loaded = ctx.enter_context(nc.semaphore("x_loaded"))
        conditioning(nc, k, dram)
        routing(nc, k, dram)
        recurrences(nc, k, dram, 0, None)
        experts(nc, k, dram, 0)
        combine(nc, k, dram, 0)
        if NM == 2:
            recurrences(nc, k, dram, 1, 0)
            experts(nc, k, dram, 1)
            combine(nc, k, dram, 1)
        else:
            with nc.Fori(1, NM) as m:
                recurrences(nc, k, dram, m, m - 1)
                experts(nc, k, dram, m)
                combine(nc, k, dram, m)
        recurrences(nc, k, dram, None, NM - 1)
        adapted_output(nc, k, dram, out)


def kernel(**inputs):
    import numpy as np
    import concourse.bacc as bacc
    from concourse.bass_utils import run_bass_kernel_spmd

    def features_first(a, *axes):
        a = np.ascontiguousarray(a)
        for ax in sorted((x % a.ndim for x in axes), reverse=True):
            s = a.shape
            a = a.reshape(s[:ax] + (4, 4, 32) + s[ax + 1:])
            a = np.moveaxis(a, ax + 1, ax)
            a = a.reshape(s[:ax] + (4, 128) + s[ax + 1:])
        return a

    def moving(w):
        return np.ascontiguousarray(features_first(w, 0).transpose(1, 0, 2))

    def stationary(w):
        return np.ascontiguousarray(features_first(w, 0, 1).transpose(1, 0, 2, 3))

    def vector(v):
        return features_first(v, 0).T

    a = {n: np.asarray(v) for n, v in inputs.items()}
    w0 = a["L0_cond_W"]
    x = features_first(a["x"], 2).transpose(3, 1, 2, 0)
    wk = features_first(a["L1_cond_w_key"], 1).reshape(E, KC, P, FC, P).transpose(0, 2, 1, 3, 4)
    wv = features_first(a["L1_cond_w_value"], 2).reshape(E, FC, P, KC * P).transpose(0, 2, 1, 3)
    w2 = features_first(a["L3_cond_w2"], 0).reshape(KC, P, 2, KC, KC, 32, RANK)
    w2 = w2.transpose(1, 2, 6, 0, 4, 3, 5).reshape(P, NPIECE, KC, D)
    b2 = a["L3_cond_b2"].reshape(2, 4, 4, 32, RANK).transpose(0, 4, 2, 1, 3).reshape(1, NPIECE * D)
    arrays = {
        "x": x.reshape(P, T * S),
        "cond": features_first(a["cond_1024"], 1).transpose(2, 1, 0).reshape(P, S),
        "tok": a["itok_BxS_2_50255"].reshape(NT, P).T,
        "wh": moving(w0[:, :D].T),
        "wz": stationary(w0[:, D:].T),
        "l0v": np.stack([vector(a["L0_cond_b"]), vector(a["L0_cond_alpha"])], 1),
        "maa": np.stack([vector(a["L1_cond_time_maa_k"]), vector(a["L1_cond_time_maa_r"])], 1),
        "w_recept": stationary(a["L1_cond_w_recept"].T),
        "w_key": wk,
        "w_value": wv,
        "ug": np.stack([moving(a["L2_cond_" + n]) for n in ("U_z", "U_r", "U")]),
        "wg": np.stack([stationary(a["L2_cond_" + n]) for n in ("W_z", "W_r", "W")]),
        "cg": np.stack([stationary(a["L2_cond_" + n]) for n in ("C_z", "C_r", "C")]),
        "bgru": np.stack([vector(a["L2_cond_" + n]) for n in ("b_z", "b_r", "b")], 1),
        "base": stationary(a["L3_cond_base_layer"]).reshape(P, KC, D),
        "w1": stationary(a["L3_cond_w1"]),
        "w2": w2,
        "b2": np.broadcast_to(b2, (B, NPIECE * D)),
        "lnb": np.stack([vector(a["L3_cond_" + n]) for n in ("ln_g", "ln_b", "b1")], 1),
    }
    arrays = {f"in_{n}": np.ascontiguousarray(v) for n, v in arrays.items()}
    nc = bacc.Bacc("TRN2", target_bir_lowering=False, num_devices=1)
    dram = {n[3:]: nc.dram_tensor(n, v.shape, mybir.dt.from_np(v.dtype), kind="ExternalInput").ap() for n, v in arrays.items()}
    out = nc.dram_tensor("out", (P, T * S), F32, kind="ExternalOutput").ap()
    cond_resid_program(nc, dram, out)
    got = run_bass_kernel_spmd(nc, [arrays], core_ids=[0]).results[0]["out"]
    return np.ascontiguousarray(np.asarray(got).reshape(4, 32, T, KC, B).transpose(4, 2, 0, 3, 1).reshape(B, T, D))
```

```python
import concourse.bass as bass
from concourse import mybir
from contextlib import ExitStack

F32 = mybir.dt.float32
BF16 = mybir.dt.bfloat16
I32 = mybir.dt.int32
ALU = mybir.AluOpType
ACT = mybir.ActivationFunctionType
AX_X = mybir.AxisListType.X

P = 128
B = 2
T = 2048
D = 512
NG = 4
KC = D // P
S = KC * B
TC = 256
NCH = T // TC
TOKC = TC * B
U = 32
HB = U // 2
NBLK = TC // U
NM = 4
CM = NCH // NM
E = 16
F = 1024
FC = F // P
CAP = B * T // E
PASSES = CAP // P
FH = F // 512
NTOK = B * T
NT = NTOK // P
Q = NT // B // NM
TPC = TOKC // P
TH = TC // P
RANK = 8
LN_EPS = 1e-5
NPIECE = 2 * D * RANK // D
OT = (NM - 1) * TC // NBLK
ADAPT_AT = 8
HASH = 5099 % E


def clear_semaphores(nc, sems):
    with nc.Block() as block:
        @block.vector
        def _(dve):
            for sem in sems:
                dve.sem_clear(sem)


def steps8(t, n):
    return t[:, n * S:(n + 1) * S]


def grouped(t):
    return t.rearrange("p (c b) -> p c b", b=B)


def turned(t):
    return t[:, 0:P].rearrange("p (c r) -> p c r", c=KC)[:, :, 0:B]


def load_leaky(sp, k, dram):
    sp.dma_start(k.wz, dram["wz"]).then_inc(k.leaky_in, 16)
    sp.dma_start(k.wh, dram["wh"]).then_inc(k.leaky_in, 16)
    sp.dma_start(k.vecs[:], dram["l0v"]).then_inc(k.leaky_in, 16)


def load_gru(sp, k, dram):
    for g in range(3):
        sp.dma_start(k.wg[:, g], dram["wg"][g]).then_inc(k.gru_in, 16)
    for g in range(3):
        sp.dma_start(k.ug[:, g], dram["ug"][g]).then_inc(k.gru_in, 16)


def seed(dve, bank, x):
    return dve.transpose(bank[:, 0:P], grouped(x).unsqueeze(2).to_broadcast([P, KC, 32 // B, B]))


def wait_alone(k, engine, sem, value):
    engine.wait_ge(sem, value)
    engine.sem_inc(k.passed, 1)


def matvec(pe, bank, w, h):
    for k in range(KC):
        for j in range(NG):
            last = pe.matmul(bank[32 * j:32 * j + B, 0:P], h[:, k, :], w[:, k, j * P:(j + 1) * P],
                             start=False, stop=(k == KC - 1), tile_position=(0, 32 * j),
                             skip_group_check=True)
    return last


def chunk_steps(a, c):
    return a[:, bass.ds(c * (TC * S) + S, TC * S)].rearrange("p (t c b) -> p t c b", c=KC, b=B)


def minus_previous(dve, dx, k, now, c):
    dve.tensor_tensor(dx[:, 0], k.before[:, bass.ds(c * S, S)].rearrange("p (c b) -> p c b", b=B), now[:, 0], ALU.subtract)
    return dve.tensor_tensor(dx[:, 1:TC], now[:, 0:TC - 1], now[:, 1:TC], ALU.subtract)


def conditioning(nc, k, dram):
    with ExitStack() as ctx:
        sb = lambda n, s, d=F32: ctx.enter_context(nc.sbuf_tensor(n, s, d))
        sems = []

        def sem(n):
            sems.append(ctx.enter_context(nc.semaphore(n)))
            return sems[-1]

        cw = sb("cond_w", [P, 3, KC, KC, P])
        w1 = sb("ada_w1", [P, KC, KC, P])
        lnb = sb("ln_gb1", [P, 3, KC])
        ones = sb("ones", [P, P])
        cen = sb("centred", [P, S])
        sq = sb("squares", [P, S])
        st = sb("stats", [P, 8])
        ae = sb("ada", [P, S])
        hp = sb("hidden_pre", [P, S])
        hid = k.hidden
        loads = sem("c_loads")
        v, pes, acts = sem("c_dve"), sem("c_pe"), sem("c_act")
        bank = k.banks
        block = ctx.enter_context(nc.Block())

        @block.sync
        def _(sp):
            sp.dma_start(k.A[:, 0:S], dram["cond"]).then_inc(loads, 16)
            sp.dma_start(lnb[:], dram["lnb"]).then_inc(loads, 16)
            sp.dma_start(k.bgru[:], dram["bgru"]).then_inc(loads, 16)
            sp.dma_start(w1[:], dram["w1"]).then_inc(loads, 16)
            for g in range(3):
                sp.dma_start(cw[:, g], dram["cg"][g]).then_inc(loads, 16)
            for c in range(NCH):
                sp.dma_start(k.A[:, S + c * TC * S:S + (c + 1) * TC * S],
                             dram["x"][:, c * TC * S:(c + 1) * TC * S]).then_inc(k.x_loaded, 16)

        @block.vector
        def _(dve):
            n = [0]

            def step(ins):
                n[0] += 1
                ins.then_inc(v, 1)
                dve.wait_ge(v, n[0])

            step(dve.memset(ones[:], 1.0))
            dve.wait_ge(loads, 16 * 7)
            dve.wait_ge(pes, 1)
            step(dve.tensor_copy(st[:, 0:2], bank[0][:, 0:2]))
            step(dve.tensor_scalar(st[:, 2:4], st[:, 0:2], 1.0 / D, None, ALU.mult))
            for b in range(B):
                step(dve.tensor_scalar(grouped(cen[:])[:, :, b], grouped(k.A[:, 0:S])[:, :, b], st[:, 2 + b:3 + b], None, ALU.subtract))
            step(dve.tensor_tensor(sq[:], cen[:], cen[:], ALU.mult))
            dve.wait_ge(pes, 2)
            step(dve.tensor_scalar(st[:, 4:6], bank[1][:, 0:2], 1.0 / D, LN_EPS, ALU.mult, ALU.add))
            dve.wait_ge(acts, 1)
            step(dve.reciprocal(st[:, 6:8], st[:, 0:2]))
            for b in range(B):
                step(dve.tensor_scalar(grouped(ae[:])[:, :, b], grouped(cen[:])[:, :, b], st[:, 6 + b:7 + b], None, ALU.mult))
            for b in range(B):
                step(dve.tensor_tensor(grouped(ae[:])[:, :, b], grouped(ae[:])[:, :, b], lnb[:, 0, :], ALU.mult))
            for b in range(B):
                step(dve.tensor_tensor(grouped(ae[:])[:, :, b], grouped(ae[:])[:, :, b], lnb[:, 1, :], ALU.add))
            for g in range(3):
                dve.wait_ge(pes, 3 + g)
                for b in range(B):
                    step(dve.tensor_tensor(grouped(k.vg[:, g])[:, :, b], grouped(bank[2 + g][:, 0:S])[:, :, b], k.bgru[:, g, :], ALU.add))
            dve.wait_ge(pes, 6)
            for b in range(B):
                step(dve.tensor_tensor(grouped(hp[:])[:, :, b], grouped(bank[5][:, 0:S])[:, :, b], lnb[:, 2, :], ALU.add))

        @block.scalar
        def _(act):
            act.wait_ge(v, 7)
            act.activation(st[:, 0:2], st[:, 4:6], ACT.Sqrt).then_inc(acts, 1)
            act.wait_ge(v, 22)
            act.activation(hid[:], hp[:], ACT.Gelu).then_inc(acts, 1)

        @block.tensor
        def _(pe):
            def over_features(out, lhs, rhs):
                for c in range(KC):
                    last = pe.matmul(out, lhs(c), rhs(c), start=(c == 0), stop=(c == KC - 1))
                return last

            pe.wait_ge(v, 1)
            pe.wait_ge(loads, 16 * 7)
            cond = grouped(k.A[:, 0:S])
            over_features(bank[0][:, 0:2], lambda c: ones[:], lambda c: cond[:, c, :]).then_inc(pes, 1)
            pe.wait_ge(v, 6)
            over_features(bank[1][:, 0:2], lambda c: ones[:], lambda c: grouped(sq[:])[:, c, :]).then_inc(pes, 1)
            for g in range(3):
                for o in range(KC):
                    last = over_features(bank[2 + g][:, o * B:(o + 1) * B], lambda c: cw[:, g, c, o, :], lambda c: cond[:, c, :])
                last.then_inc(pes, 1)
            pe.wait_ge(v, 14)
            for o in range(KC):
                last = over_features(bank[5][:, o * B:(o + 1) * B], lambda c: w1[:, c, o, :], lambda c: grouped(ae[:])[:, c, :])
            last.then_inc(pes, 1)
    clear_semaphores(nc, sems)


def routing(nc, k, dram):
    with ExitStack() as ctx:
        sb = lambda n, s, d=F32: ctx.enter_context(nc.sbuf_tensor(n, s, d))
        sems = []

        def sem(n):
            sems.append(ctx.enter_context(nc.semaphore(n)))
            return sems[-1]

        tok = sb("tok", [P, NT], I32)
        ei = sb("expert_i", [P, NT], I32)
        ef = sb("expert", [P, NT])
        iota_e = sb("iota_e", [P, E], I32)
        iota_n = sb("iota_n", [P, NT], I32)
        iota_ef = sb("iota_ef", [P, E])
        trash = sb("trash", [P, NT])
        hot = sb("one_hot", [P, NT, E])
        tot = sb("totals", [P, NT, E])
        run = [sb("run_a", [P, NT, E]), sb("run_b", [P, NT, E])]
        pos = sb("pos", [P, NT])
        keep = sb("keep", [P, NT])
        slot = sb("slot", [P, NT])
        dif = sb("dif", [P, NT])
        rank = sb("rank", [P, NT])
        late = sb("late", [P, NT])
        pairs = sb("pairs_f", [1, 2 * NM])
        upto = sb("upto", [P, P])
        ones = sb("r_ones", [P, P])
        tok_in, made, v, counted, late_made, late_counted = (sem("r_" + n) for n in (
            "tok", "made", "dve", "counted", "late_made", "late_counted"))
        block = ctx.enter_context(nc.Block())

        @block.sync
        def _(sp):
            sp.dma_start(tok[:], dram["tok"]).then_inc(tok_in, 16)
            load_leaky(sp, k, dram)
            sp.wait_ge(k.x_loaded, 16 * NCH)

        @block.gpsimd
        def _(pool):
            pool.iota(iota_e[:], pattern=[[1, E]], base=0, channel_multiplier=0).then_inc(made, 1)
            pool.iota(iota_n[:], pattern=[[P, NT]], base=E * CAP, channel_multiplier=1).then_inc(made, 1)
            pool.memset(upto[:], 1.0).then_inc(made, 1)
            pool.memset(k.ident[:], 0.0).then_inc(made, 1)
            pool.memset(ones[:], 1.0).then_inc(made, 1)
            pool.wait_ge(made, 5)
            pool.affine_select(out=upto[:], in_=upto[:], pattern=[[1, P]], compare_op=ALU.is_ge, fill=0.0, base=0, channel_multiplier=-1).then_inc(made, 1)
            pool.affine_select(out=k.ident[:], in_=k.ident[:], pattern=[[-1, P]], compare_op=ALU.not_equal, fill=1.0, base=0, channel_multiplier=1).then_inc(made, 1)

        @block.vector
        def _(dve):
            n = [0]

            def step(ins):
                n[0] += 1
                ins.then_inc(v, 1)
                dve.wait_ge(v, n[0])

            dve.wait_ge(tok_in, 16)
            dve.wait_ge(made, 5)
            step(dve.tensor_scalar(ei[:], tok[:], E - 1, None, ALU.bitwise_and))
            step(dve.tensor_scalar(ei[:], ei[:], HASH, None, ALU.mult))
            step(dve.tensor_scalar(ei[:], ei[:], E - 1, None, ALU.bitwise_and))
            step(dve.tensor_copy(ef[:], ei[:]))
            step(dve.tensor_copy(iota_ef[:], iota_e[:]))
            step(dve.tensor_copy(trash[:], iota_n[:]))
            step(dve.tensor_tensor(hot[:], ef[:].unsqueeze(2).to_broadcast([P, NT, E]), iota_ef[:].unsqueeze(1).to_broadcast([P, NT, E]), ALU.is_equal))
            dve.wait_ge(counted, 1)
            step(dve.tensor_copy(tot[:].rearrange("p n e -> p (n e)"), k.banks[1][:, :]))
            step(dve.tensor_copy(run[0][:], tot[:]))
            a = 0
            d = 1
            while d < NT:
                step(dve.tensor_copy(run[1 - a][:, 0:d], run[a][:, 0:d]))
                step(dve.tensor_tensor(run[1 - a][:, d:NT], run[a][:, d:NT], run[a][:, 0:NT - d], ALU.add))
                a = 1 - a
                d *= 2
            within = k.banks[0][:, :].rearrange("p (n e) -> p n e", e=E)

            def place(out, before):
                step(dve.tensor_tensor(before[:], before[:], within, ALU.add))
                step(dve.tensor_tensor(before[:], before[:], hot[:], ALU.mult))
                step(dve.tensor_reduce(out[:], before[:], AX_X, ALU.add))

            step(dve.tensor_tensor(run[a][:], run[a][:], tot[:], ALU.subtract))
            place(pos, run[a])
            step(dve.tensor_scalar(keep[:], pos[:], float(CAP), None, ALU.is_le))
            tiles = lambda t: t[:].rearrange("p (g q) e -> p g q e", q=Q)
            a = 0
            d = 1
            step(dve.tensor_copy(run[0][:], tot[:]))
            while d < Q:
                step(dve.tensor_copy(tiles(run[1 - a])[:, :, 0:d], tiles(run[a])[:, :, 0:d]))
                step(dve.tensor_tensor(tiles(run[1 - a])[:, :, d:Q], tiles(run[a])[:, :, d:Q], tiles(run[a])[:, :, 0:Q - d], ALU.add))
                a = 1 - a
                d *= 2
            for q in range(Q):
                step(dve.tensor_tensor(tiles(run[1 - a])[:, NM:2 * NM, q], tiles(run[a])[:, NM:2 * NM, q], tiles(run[a])[:, 0:NM, Q - 1], ALU.add))
            step(dve.tensor_copy(run[1 - a][:, 0:NT // B], run[a][:, 0:NT // B]))
            a = 1 - a
            step(dve.tensor_tensor(run[a][:], run[a][:], tot[:], ALU.subtract))
            place(rank, run[a])
            step(dve.tensor_scalar(late[:], rank[:], float(P), None, ALU.is_gt))
            step(dve.tensor_scalar(slot[:], ef[:], float(P), -1.0, ALU.mult, ALU.add))
            step(dve.tensor_tensor(slot[:], slot[:], rank[:], ALU.add))
            step(dve.tensor_scalar(dif[:], late[:], float((E - 1) * P), None, ALU.mult))
            step(dve.tensor_tensor(slot[:], slot[:], dif[:], ALU.add))
            dve.tensor_tensor(late[:], late[:], keep[:], ALU.mult).then_inc(late_made, 1)
            step(dve.tensor_tensor(dif[:], slot[:], trash[:], ALU.subtract))
            step(dve.tensor_tensor(dif[:], dif[:], keep[:], ALU.mult))
            step(dve.tensor_tensor(dif[:], dif[:], trash[:], ALU.add))
            step(dve.tensor_copy(k.put[:], dif[:]))
            step(dve.tensor_scalar(slot[:], slot[:], -float(E * CAP), None, ALU.add))
            step(dve.tensor_tensor(slot[:], slot[:], keep[:], ALU.mult))
            step(dve.tensor_scalar(slot[:], slot[:], float(E * CAP), None, ALU.add))
            step(dve.tensor_copy(k.get[:], slot[:]))
            dve.wait_ge(late_counted, 1)
            step(dve.tensor_reduce(pairs[:].rearrange("p (b m) -> p b m", b=B),
                                   k.banks[2][0:1, 0:NT].rearrange("p (b m q) -> p b m q", b=B, m=NM), AX_X, ALU.add))
            step(dve.tensor_tensor(pairs[:, 0:NM], pairs[:, 0:NM], pairs[:, NM:2 * NM], ALU.add))
            step(dve.tensor_scalar(pairs[:, 0:NM], pairs[:, 0:NM], 1.0, None, ALU.min))
            step(dve.tensor_scalar(pairs[:, 0:NM], pairs[:, 0:NM], float(E // 2), float(E // 2), ALU.mult, ALU.add))
            step(dve.tensor_copy(k.pairs[:], pairs[:, 0:NM]))

        @block.tensor
        def _(pe):
            pe.wait_ge(made, 7)
            pe.wait_ge(v, 7)
            flat = hot[:].rearrange("p n e -> p (n e)")
            pe.matmul(k.banks[0][:, :], upto[:], flat, start=True, stop=True)
            pe.matmul(k.banks[1][:, :], ones[:], flat, start=True, stop=True).then_inc(counted, 1)
            pe.wait_ge(late_made, 1)
            pe.matmul(k.banks[2][:, 0:NT], ones[:], late[:], start=True, stop=True).then_inc(late_counted, 1)
    clear_semaphores(nc, sems)


assert NPIECE == CM * NBLK
assert OT * CM * NBLK == (NM - 1) * CM * TC and KC * (KC * B // 2) <= U // 2


def recurrences(nc, k, dram, leaky, gru, out=None):
    Z, R, H = range(3)
    with_l, with_g = leaky is not None, gru is not None
    tag = k.next_run()
    with ExitStack() as ctx:
        sb = lambda n, s, d=F32: ctx.enter_context(nc.sbuf_tensor(n + tag, s, d))
        sems = []

        def sem(n):
            sems.append(ctx.enter_context(nc.semaphore(n + tag)))
            return sems[-1]

        ready = sem("s_ready")
        if with_l:
            wh, wz, vecs = k.wh, k.wz, k.vecs
            leak = sb("leak", [P, S])
            xz = sb("l_xz", [P, TC * S])
            xz_ring = sb("l_xz_ring", [P, U * S])
            x_ring = sb("l_x_ring", [P, U * S])
            tl = sb("l_t", [P, P])
            gl, gx, hl, up = (sb(n, [P, S]) for n in ("l_gate", "l_gate_x", "l_h_leak", "l_update"))
            l_proj, l_projected, l_staged, l_seeded, l_ps, l_pre, l_gate, l_chain, l_h, l_added = (sem("l_" + n) for n in (
                "proj", "projected", "staged", "seeded", "ps", "pre", "gate", "chain", "h", "added"))
            bl = [k.banks[7], k.banks[3]]
        if with_g:
            ug, wg = k.ug, k.wg
            xg = sb("g_x", [P, 3, TC * S])
            g_ring = sb("g_ring", [P, 3, U * S])
            tz, tr, th = (sb(n, [P, P]) for n in ("z_t", "r_t", "h_t"))
            gz, gr, gh, rh, zh, keep = (sb(n, [P, S]) for n in ("gate_z", "gate_r", "cand", "rh", "z_cand", "keep_h"))
            g_proj, g_projected, g_staged, r_seeded, z_seeded, h_seeded, g_added = (sem("g_" + n) for n in (
                "proj", "projected", "staged", "r_seeded", "z_seeded", "h_seeded", "added"))
            r_ps, z_ps, h_ps, pre_r, pre_z, pre_h, r_gate, z_gate, cand, rh_ready, g_chain, g_h = (sem("g_" + n) for n in (
                "r_ps", "z_ps", "h_ps", "pre_r", "pre_z", "pre_h", "r_gate", "z_gate", "cand", "rh_ready", "chain", "h"))
            bz, br, bh = ([k.banks[4 + n], k.banks[n]] for n in range(3))
        warm = sb("warm", [P, D], BF16)
        opened = sem("s_opened")
        adapter = with_l and not with_g
        if adapter:
            w2 = sb("ada_w2", [P, KC, D])
            b2 = sb("ada_b2", [B, D])
            xw = sb("ada_xw", [B, D])
            zeros = sb("zeros", [P, D])
            zeros_made, zero_out, w2_in, xw_ps, xw_ready, xw_out = (sem("c_" + n) for n in (
                "zeros_made", "zero_out", "w2_in", "xw_ps", "xw_ready", "xw_out"))
        outputs = with_g and not with_l
        if outputs:
            o_sb = sb("out_early", [P, OT * S])
            early_ps, early_ready, early_stored = (sem("o_" + n) for n in ("early_ps", "early_ready", "early_stored"))

        def early_steps(c, i):
            return k.A[:, bass.ds(S + (c * NBLK + i) * (OT * S), OT * S)].rearrange("p (t c b) -> p t c b", c=KC, b=B)

        block = ctx.enter_context(nc.Block())

        if outputs:
            @block.sync
            def _(sp):
                with sp.Fori(0, CM * NBLK) as n:
                    sp.wait_ge(early_ready, n * KC + KC + 1)
                    sp.dma_start(out[:, bass.ds(n * (OT * S), OT * S)], o_sb[:]).then_inc(early_stored, 16)
                sp.wait_ge(early_stored, 16 * (CM * NBLK) + 16)

        if adapter:
            @block.sync
            def _(sp):
                def load_piece(p):
                    sp.dma_start(w2[:], dram["w2"][:, bass.ds(p, 1)].rearrange("p o k n -> p (o k) n")).then_inc(w2_in, 16)
                    sp.dma_start(b2[:], dram["b2"][:, bass.ds(p * D, D)]).then_inc(w2_in, 16)

                def clear_slots(p):
                    for name in ("expert_in", "expert_out"):
                        sp.dma_start(dram[name][bass.ds(p * (2 * P), 2 * P), :].rearrange("(q p) d -> p q d", p=P),
                                     zeros[:].unsqueeze(1).to_broadcast([P, 2, D])).then_inc(zero_out, 16)

                load_piece(0)
                sp.wait_ge(zeros_made, 1)
                sp.dma_start(dram["expert_out"][E * CAP:E * CAP + 1, :], zeros[0:1, :]).then_inc(zero_out, 16)
                with sp.Fori(0, NPIECE - 1) as p:
                    clear_slots(p)
                    sp.wait_ge(xw_ready, p + 1)
                    sp.dma_start(dram["xw"][:, bass.ds(p, 1), :].rearrange("b o n -> b (o n)"), xw[:]).then_inc(xw_out, 16)
                    load_piece(p + 1)
                clear_slots(NPIECE - 1)
                sp.wait_ge(xw_ready, NPIECE)
                sp.dma_start(dram["xw"][:, NPIECE - 1, :], xw[:]).then_inc(xw_out, 16)
                sp.wait_ge(xw_out, 16 * NPIECE + 16)
                sp.wait_ge(zero_out, 16 * (2 * NPIECE + 1))

        def weights_are_in(engine):
            if with_l:
                engine.wait_ge(k.leaky_in, 16 * 3)
            if with_g:
                engine.wait_ge(k.gru_in, 16 * 6)

        @block.tensor
        def _(pe):
            weights_are_in(pe)
            pe.wait_ge(ready, 1)
            for n in range(4, 8):
                last = pe.matmul(k.banks[n][:, :], warm[:, 0:P], warm[:, :], start=True, stop=True)
            last.then_inc(opened, 1)
            with pe.Fori(0, CM) as c:
                if with_l:
                    pe.wait_ge(l_h, c * TC + 1)
                if with_g:
                    pe.wait_ge(g_h, c * TC + 1)
                if with_l:
                    for o in range(KC):
                        if with_g:
                            pe.wait_ge(g_projected, c * (3 * KC) + KC)
                        for q in range(KC):
                            last = pe.matmul(k.banks[o][:, :], wz[:, q, o, :], chunk_steps(k.A, leaky * CM + c)[:, :, q, :],
                                             start=(q == 0), stop=(q == KC - 1))
                        last.then_inc(l_proj, 1)
                if with_g:
                    for g in range(3):
                        for o in range(KC):
                            if with_l and g == 0:
                                pe.wait_ge(l_projected, c * KC + o + 1)
                            pe.wait_ge(g_projected, c * (3 * KC) + g * KC + o + 1)
                            for q in range(KC):
                                last = pe.matmul(k.banks[o][:, :], wg[:, g, q, o, :], chunk_steps(k.A, gru * CM + c)[:, :, q, :],
                                                 start=(q == 0), stop=(q == KC - 1))
                            last.then_inc(g_proj, 1)
                with pe.Fori(0, NBLK) as i:
                    for u in range(U):
                        st = c * TC + i * U + u
                        if with_l:
                            pe.wait_ge(l_seeded, st + c + 1)
                            pe.wait_ge(l_h, st + 1)
                            matvec(pe, bl[u % 2], wh, grouped(steps8(k.h_leaky, (u - 1) % U))).then_inc(l_ps, 1)
                        if with_g:
                            h = grouped(steps8(k.h_gru, (u - 1) % U))
                            pe.wait_ge(r_seeded, st + c + 1)
                            pe.wait_ge(g_h, st + 1)
                            matvec(pe, br[u % 2], ug[:, R], h).then_inc(r_ps, 1)
                            pe.wait_ge(z_seeded, st + c + 1)
                            matvec(pe, bz[u % 2], ug[:, Z], h).then_inc(z_ps, 1)
                            pe.wait_ge(h_seeded, st + c + 1)
                            pe.wait_ge(rh_ready, st + 1)
                            matvec(pe, bh[u % 2], ug[:, H], grouped(rh[:])).then_inc(h_ps, 1)
                        if adapter and u // KC == ADAPT_AT // KC:
                            q = u % KC
                            if q == 0:
                                pe.wait_ge(w2_in, 32 * (c * NBLK + i) + 32)
                            last = pe.matmul(k.banks[6][0:B, :], grouped(k.hidden[:])[:, q, :], w2[:, q, :], start=(q == 0), stop=(q == KC - 1))
                            if q == KC - 1:
                                last.then_inc(xw_ps, 1)
                        elif outputs and u % (2 * KC) < KC:
                            o = u // (2 * KC)
                            if u % KC == 0:
                                pe.wait_ge(early_ready, (c * NBLK + i) * KC + o + 1)
                            for n in range(2 * (u % KC), 2 * (u % KC) + 2):
                                b, q = n // KC, n % KC
                                last = pe.matmul(k.banks[7][:, b * OT:(b + 1) * OT], k.layer[:, b, q, o * P:(o + 1) * P],
                                                 early_steps(c, i)[:, :, q, b], start=(n == 0), stop=(q == KC - 1), skip_group_check=True)
                            if u % KC == KC - 1:
                                last.then_inc(early_ps, 1)
                        elif not (with_l and with_g):
                            for _ in range(3):
                                pe.matmul(k.banks[5 if with_l else 3][0:B, :], warm[:, 0:B], warm[:, :], start=True, stop=True)

        @block.scalar
        def _(act):
            weights_are_in(act)
            act.wait_ge(ready, 1)
            if with_g:
                act.sem_inc(g_projected, KC)
            with act.Fori(0, CM) as c:
                if with_l:
                    act.wait_ge(l_added, c * (2 * NBLK) + 2)
                    for o in range(KC):
                        act.wait_ge(l_proj, c * KC + o + 1)
                        act.activation(xz[:].rearrange("p (t c b) -> p t c b", c=KC, b=B)[:, :, o, :],
                                       k.banks[o][:, :].rearrange("p (t b) -> p t b", b=B),
                                       ACT.Identity, bias=vecs[:, 0, o:o + 1]).then_inc(l_projected, 1)
                if with_g:
                    act.wait_ge(g_added, c * (2 * NBLK) + 2)
                    for g in range(3):
                        for o in range(KC):
                            act.wait_ge(g_proj, c * (3 * KC) + g * KC + o + 1)
                            for b in range(B):
                                last = act.activation(xg[:, g].rearrange("p (t c b) -> p t c b", c=KC, b=B)[:, :, o, b],
                                                      k.banks[o][:, :].rearrange("p (t b) -> p t b", b=B)[:, :, b],
                                                      ACT.Identity, bias=k.vg[:, g, o * B + b:o * B + b + 1])
                            last.then_inc(g_projected, 1)
                with act.Fori(0, NBLK) as i:
                    for u in range(U):
                        st = c * TC + i * U + u
                        if with_l:
                            act.wait_ge(l_pre, st + 1)
                            act.activation(grouped(gl[:]), turned(tl), ACT.Sigmoid).then_inc(l_gate, 1)
                            act.wait_ge(l_chain, 3 * st + 3)
                            if u % HB == 0:
                                act.wait_ge(l_added, (c * NBLK + i) * 2 + u // HB + 1)
                            act.activation(steps8(k.h_leaky, u), up[:], ACT.Tanh).then_inc(l_h, 1)
                        if with_g:
                            act.wait_ge(pre_r, st + 1)
                            act.activation(grouped(gr[:]), turned(tr), ACT.Sigmoid).then_inc(r_gate, 1)
                            act.wait_ge(pre_z, st + 1)
                            act.activation(grouped(gz[:]), turned(tz), ACT.Sigmoid).then_inc(z_gate, 1)
                            act.wait_ge(pre_h, st + 1)
                            act.activation(grouped(gh[:]), turned(th), ACT.Tanh).then_inc(cand, 1)

        @block.gpsimd
        def _(pool):
            def halves():
                for half in range(2):
                    yield half, half * HB * S, (half + 1) * HB * S

            def span_steps(span, c, at):
                return k.A[:, bass.ds(S + (span * CM + c) * (TC * S) + at, HB * S)]

            def add_half(c, i, half, a, b):
                through = c * TC + i * U + (half + 1) * HB + 1
                for on, span, h, ring, added in recurring:
                    if on:
                        pool.wait_ge(h, through)
                        here = span_steps(span, c, i * (U * S) + a)
                        pool.tensor_tensor(here, here, ring[:, a:b], ALU.add).then_inc(added, 1)

            recurring = [(with_l, leaky, l_h if with_l else None, k.h_leaky, l_added if with_l else None),
                         (with_g, gru, g_h if with_g else None, k.h_gru, g_added if with_g else None)]
            if with_l:
                pool.sem_inc(l_added, 2)
            if with_g:
                pool.sem_inc(g_added, 2)
            with pool.Fori(0, CM) as c:
                for half, a, b in halves():
                    if with_l:
                        if half == 0:
                            wait_alone(k, pool, l_projected, (c + 1) * KC)
                        pool.tensor_copy(xz_ring[:, a:b], xz[:, a:b]).then_inc(l_staged, 1)
                        pool.tensor_copy(x_ring[:, a:b], span_steps(leaky, c, a)).then_inc(l_staged, 1)
                    if with_g:
                        if half == 0:
                            wait_alone(k, pool, g_projected, (c + 1) * (3 * KC) + KC)
                        pool.tensor_copy(g_ring[:, :, a:b], xg[:, :, a:b]).then_inc(g_staged, 1)
                with pool.Fori(0, NBLK - 1) as i:
                    for half, a, b in halves():
                        add_half(c, i, half, a, b)
                        ahead = (i + 1) * (U * S) + a
                        if with_l:
                            pool.tensor_copy(xz_ring[:, a:b], xz[:, bass.ds(ahead, HB * S)]).then_inc(l_staged, 1)
                            pool.tensor_copy(x_ring[:, a:b], span_steps(leaky, c, ahead)).then_inc(l_staged, 1)
                        if with_g:
                            pool.tensor_copy(g_ring[:, :, a:b], xg[:, :, bass.ds(ahead, HB * S)]).then_inc(g_staged, 1)
                for half, a, b in halves():
                    add_half(c, NBLK - 1, half, a, b)
                    if half == 0:
                        if with_l:
                            pool.sem_inc(l_staged, 2)
                        if with_g:
                            pool.sem_inc(g_staged, 1)

        @block.vector
        def _(dve):
            dve.memset(warm[:], 0.0)
            if outputs:
                dve.sem_inc(early_ready, 1)
                dve.sem_inc(early_stored, 16)
            if adapter:
                dve.memset(zeros[:], 0.0).then_inc(zeros_made, 1)
                dve.sem_inc(xw_out, 16)
            if with_l:
                dve.wait_ge(k.leaky_in, 16 * 3)
                for b in range(B):
                    dve.tensor_scalar(grouped(leak[:])[:, :, b], vecs[:, 1, :], -1.0, 1.0, ALU.mult, ALU.add)
                dve.sem_inc(l_h, 1)
            if with_g:
                dve.sem_inc(g_h, 1)
            if with_l and isinstance(leaky, int) and leaky == 0:
                dve.memset(steps8(k.h_gru, U - 1), 0.0)
                dve.tensor_copy(k.before[:, 0:S], k.A[:, 0:S])
                dve.tensor_copy(steps8(k.h_leaky, U - 1), k.A[:, 0:S]).then_inc(ready, 1)
            else:
                dve.memset(rh[:], 0.0).then_inc(ready, 1)
            dve.wait_ge(ready, 1)

            def seed_gate(gate, bank, seeded, u):
                seed(dve, bank[u % 2], steps8(g_ring[:, gate], u % U)).then_inc(seeded, 1)

            dve.wait_ge(opened, 1)
            with dve.Fori(0, CM) as c:
                if with_l:
                    dve.wait_ge(l_staged, c * (4 * NBLK + 2) + 2)
                    seed(dve, bl[0], steps8(xz_ring, 0)).then_inc(l_seeded, 1)
                if with_g:
                    dve.wait_ge(g_staged, c * (2 * NBLK + 1) + 1)
                    for gate, bank, seeded in ((R, br, r_seeded), (Z, bz, z_seeded), (H, bh, h_seeded)):
                        seed_gate(gate, bank, seeded, 0)
                with dve.Fori(0, NBLK) as i:
                    for u in range(U):
                        st = c * TC + i * U + u
                        half_ends = u % HB == HB - 1
                        if with_l:
                            dve.wait_ge(l_h, st + 1)
                            dve.tensor_tensor(hl[:], steps8(k.h_leaky, (u - 1) % U), leak[:], ALU.mult).then_inc(l_chain, 1)
                            dve.wait_ge(l_ps, st + 1)
                            dve.transpose(tl[:], bl[u % 2][:, 0:P]).then_inc(l_pre, 1)
                            if half_ends:
                                dve.wait_ge(l_staged, c * (4 * NBLK + 2) + i * 4 + 2 * (u // HB) + 4)
                            seed(dve, bl[(u + 1) % 2], steps8(xz_ring, (u + 1) % U)).then_inc(l_seeded, 1)
                            dve.wait_ge(l_gate, st + 1)
                            dve.tensor_tensor(gx[:], gl[:], steps8(x_ring, u), ALU.mult).then_inc(l_chain, 1)
                            dve.wait_ge(l_chain, 3 * st + 2)
                            dve.tensor_tensor(up[:], gx[:], hl[:], ALU.add).then_inc(l_chain, 1)
                        if adapter and u == ADAPT_AT + KC:
                            dve.wait_ge(xw_out, 16 * (c * NBLK + i) + 16)
                            dve.wait_ge(xw_ps, c * NBLK + i + 1)
                            dve.tensor_tensor(xw[:], k.banks[6][0:B, :], b2[:], ALU.add).then_inc(xw_ready, 1)
                        if with_g:
                            h = steps8(k.h_gru, (u - 1) % U)
                            if half_ends:
                                dve.wait_ge(g_staged, c * (2 * NBLK + 1) + i * 2 + u // HB + 2)
                            seed_gate(R, br, r_seeded, u + 1)
                            if outputs and u % (2 * KC) == KC + 1:
                                o = u // (2 * KC)
                                if o == 0:
                                    dve.wait_ge(early_stored, 16 * (c * NBLK + i) + 16)
                                dve.wait_ge(early_ps, (c * NBLK + i) * KC + o + 1)
                                dve.scalar_tensor_tensor(o_sb[:].rearrange("p (t c b) -> p b t c", c=KC, b=B)[:, :, :, o],
                                                         early_steps(c, i)[:, :, o, :].rearrange("p t b -> p b t"), 2.0,
                                                         k.banks[7][:, 0:B * OT].rearrange("p (b t) -> p b t", b=B), ALU.mult, ALU.add).then_inc(early_ready, 1)
                            dve.wait_ge(r_ps, st + 1)
                            dve.transpose(tr[:], br[u % 2][:, 0:P]).then_inc(pre_r, 1)
                            dve.wait_ge(r_gate, st + 1)
                            dve.tensor_tensor(rh[:], gr[:], h, ALU.mult).then_inc(rh_ready, 1)
                            seed_gate(Z, bz, z_seeded, u + 1)
                            dve.wait_ge(z_ps, st + 1)
                            dve.transpose(tz[:], bz[u % 2][:, 0:P]).then_inc(pre_z, 1)
                            dve.wait_ge(z_gate, st + 1)
                            dve.scalar_tensor_tensor(keep[:], gz[:], -1.0, h, ALU.add, ALU.mult).then_inc(g_chain, 1)
                            seed_gate(H, bh, h_seeded, u + 1)
                            dve.wait_ge(h_ps, st + 1)
                            dve.transpose(th[:], bh[u % 2][:, 0:P]).then_inc(pre_h, 1)
                            dve.wait_ge(cand, st + 1)
                            dve.tensor_tensor(zh[:], gz[:], gh[:], ALU.mult).then_inc(g_chain, 1)
                            dve.wait_ge(g_chain, 2 * st + 2)
                            if u % HB == 0:
                                dve.wait_ge(g_added, (c * NBLK + i) * 2 + u // HB + 1)
                            dve.tensor_tensor(steps8(k.h_gru, u), zh[:], keep[:], ALU.subtract).then_inc(g_h, 1)
    clear_semaphores(nc, sems + with_l * [k.leaky_in] + with_g * [k.gru_in])


def experts(nc, k, dram, m, recept):
    tag = k.next_run()
    with ExitStack() as ctx:
        sb = lambda n, s, d=F32: ctx.enter_context(nc.sbuf_tensor(n + tag, s, d))
        sems = []

        def sem(n):
            sems.append(ctx.enter_context(nc.semaphore(n + tag)))
            return sems[-1]

        maa = sb("maa", [P, 2, KC])
        key, val = k.key, k.val
        w_in = [sem(f"m_w_in{s}") for s in range(2)]
        maa_in, recept_in, shifted, mixed, rows_t, rows_ready, idx_ready, rows_free, xr_mixed, r_ps, r_ready = (sem("m_" + n) for n in (
            "maa_in", "recept_in", "shifted", "mixed", "rows_t", "rows_ready", "idx_ready", "rows_free", "xr_mixed", "r_ps", "r_ready"))
        with ExitStack() as c1:
            dx = c1.enter_context(nc.sbuf_tensor("dx" + tag, [P, TC, KC, B], F32))
            xk = c1.enter_context(nc.sbuf_tensor("xk" + tag, [P, KC, B, TC], F32))
            wr = c1.enter_context(nc.sbuf_tensor("w_recept" + tag, [P, KC, KC, P], F32))
            xr = c1.enter_context(nc.sbuf_tensor("xr" + tag, [P, KC, TOKC], F32))
            rows = c1.enter_context(nc.sbuf_tensor("rows" + tag, [P, TPC, D], F32))
            put = [c1.enter_context(nc.sbuf_tensor(f"put{n}" + tag, [P, 1], I32)) for n in range(TPC)]
            block = c1.enter_context(nc.Block())

            @block.sync
            def _(sp):
                sp.dma_start(maa[:], dram["maa"]).then_inc(maa_in, 16)
                sp.dma_start(wr[:], dram["w_recept"]).then_inc(recept_in, 16)
                for s in range(2):
                    sp.dma_start(key[s][:], dram["w_key"][s]).then_inc(w_in[s], 16)
                    sp.dma_start(val[s][:], dram["w_value"][s]).then_inc(w_in[s], 16)

            @block.vector
            def _(dve):
                dve.wait_ge(maa_in, 16)
                dve.sem_inc(mixed, 1)
                with dve.Fori(0, CM) as c:
                    now = chunk_steps(k.A, m * CM + c)
                    dve.tensor_copy(k.before[:, bass.ds((m * CM + c + 1) * S, S)], k.A[:, bass.ds((m * CM + c + 1) * (TC * S), S)]).then_inc(shifted, 1)
                    minus_previous(dve, dx, k, now, m * CM + c).then_inc(shifted, 1)
                    dve.wait_ge(shifted, 2 * c + 2)
                    dve.wait_ge(rows_t, c * TPC + TPC)
                    for o in range(KC):
                        last = dve.scalar_tensor_tensor(xk[:, o].rearrange("p b t -> p t b"), dx[:, :, o, :], maa[:, 0, o:o + 1],
                                                 now[:, :, o, :], ALU.mult, ALU.add)
                    last.then_inc(mixed, 1)
                    dve.wait_ge(mixed, c + 2)
                    wait_alone(k, dve, rows_free, c + 1)
                    for n in range(TPC):
                        last = dve.tensor_copy(put[n][:], k.put[:, bass.ds((m * CM + c) * TH + (n // TH) * (NT // B) + n % TH, 1)])
                    last.then_inc(idx_ready, 1)
                    dve.wait_ge(r_ps, c * KC + KC)
                    for o in range(KC):
                        last = dve.scalar_tensor_tensor(xr[:, o].rearrange("p (t b) -> p t b", b=B), dx[:, :, o, :], maa[:, 1, o:o + 1],
                                                        now[:, :, o, :], ALU.mult, ALU.add)
                    last.then_inc(xr_mixed, 1)
                    dve.wait_ge(xr_mixed, c + 1)

            @block.tensor
            def _(pe):
                pe.sem_inc(rows_t, TPC)
                pe.sem_inc(r_ps, KC)
                pe.wait_ge(recept_in, 16)
                with pe.Fori(0, CM) as c:
                    pe.wait_ge(mixed, c + 2)
                    for n in range(TPC):
                        pe.wait_ge(rows_ready, c * TPC + n + 1)
                        for o in range(KC):
                            last = pe.transpose(k.banks[n][:, o * P:(o + 1) * P], xk[:, o, n // TH, (n % TH) * P:(n % TH + 1) * P], k.ident[:])
                        last.then_inc(rows_t, 1)
                    pe.wait_ge(xr_mixed, c + 1)
                    for o in range(KC):
                        pe.wait_ge(r_ready, c * KC + o + 1)
                        for q in range(KC):
                            last = pe.matmul(k.banks[4 + o][:, :], wr[:, q, o, :], xr[:, q, :], start=(q == 0), stop=(q == KC - 1))
                        last.then_inc(r_ps, 1)

            @block.scalar
            def _(act):
                act.sem_inc(rows_ready, TPC)
                act.sem_inc(r_ready, KC)
                with act.Fori(0, CM) as c:
                    act.wait_ge(rows_free, c + 1)
                    for n in range(TPC):
                        act.wait_ge(rows_t, c * TPC + n + 1 + TPC)
                        act.activation(rows[:, n, :], k.banks[n][:, :], ACT.Copy).then_inc(rows_ready, 1)
                    for o in range(KC):
                        act.wait_ge(r_ps, c * KC + o + 1 + KC)
                        act.activation(recept[:, bass.ds(c, 1), o].rearrange("p c t b -> p (c t b)"), k.banks[4 + o][:, :], ACT.Sigmoid).then_inc(r_ready, 1)

            @block.gpsimd
            def _(pool):
                pool.sem_inc(rows_free, 1)
                with pool.Fori(0, CM) as c:
                    pool.wait_ge(idx_ready, c + 1)
                    for n in range(TPC):
                        wait_alone(k, pool, rows_ready, c * TPC + n + 1 + TPC)
                        pool.indirect_dma_start(out=dram["expert_in"][:, :], out_offset=bass.IndirectOffsetOnAxis(ap=put[n][:, 0:1], axis=0),
                                                in_=rows[:, n, :], in_offset=None).then_inc(k.scattered, 16)
                    wait_alone(k, pool, k.scattered, 16 * TPC * (m * CM + c + 1))
                    pool.sem_inc(rows_free, 1)

        with ExitStack() as c2:
            sb2 = lambda n, s: c2.enter_context(nc.sbuf_tensor(n + tag, s, F32))
            xin = [sb2(f"xin{s}", [P, D]) for s in range(2)]
            xt = sb2("xt", [P, KC, P])
            rel = [sb2(f"relu{h}", [P, 512]) for h in range(FH)]
            sq = [sb2(f"hidden_rows{h}", [P, 512]) for h in range(FH)]
            hid = sb2("hidden", [P, FC, P])
            yo = [sb2(f"yo{s}", [P, D]) for s in range(2)]
            x_in = [sem(f"m_x_in{s}") for s in range(2)]
            y_out = [sem(f"m_y_out{s}") for s in range(2)]
            x_ps, xt_ready, key_ps, rel_ready, sq_ready, hid_ps, hid_ready, val_ps, yo_ready = (
                sem("m_" + n) for n in (
                    "x_ps", "xt_ready", "key_ps", "rel_ready", "sq_ready", "hid_ps", "hid_ready", "val_ps", "yo_ready"))
            block = c2.enter_context(nc.Block())

            def pairs_of(engine):
                return engine.value_load(k.pairs[0:1, bass.ds(m, 1)], min_val=E // 2, max_val=PASSES * E // 2)

            def slots(name, item):
                return dram[name][bass.ds(item * P, P), :]

            @block.sync
            def _(sp):
                pairs = pairs_of(sp)
                for s in range(2):
                    sp.dma_start(xin[s][:], slots("expert_in", s)).then_inc(x_in[s], 16)
                with sp.Fori(0, pairs - 1) as i:
                    for s in range(2):
                        item = 2 * i + s + 2
                        sp.wait_ge(val_ps, 2 * i + s + 1)
                        sp.dma_start(key[s][:], dram["w_key"][bass.ds(item % E, 1)].rearrange("e p a b -> (e p) a b")).then_inc(w_in[s], 16)
                        sp.dma_start(val[s][:], dram["w_value"][bass.ds(item % E, 1)].rearrange("e p a b -> (e p) a b")).then_inc(w_in[s], 16)
                        sp.dma_start(xin[s][:], slots("expert_in", item)).then_inc(x_in[s], 16)

            @block.tensor
            def _(pe):
                pairs = pairs_of(pe)
                with pe.Fori(0, pairs) as i:
                    for s in range(2):
                        item = 2 * i + s
                        pe.wait_ge(x_in[s], 16 * i + 16)
                        for o in range(KC):
                            last = pe.transpose(k.banks[0][:, o * P:(o + 1) * P], xin[s][:, o * P:(o + 1) * P], k.ident[:])
                        last.then_inc(x_ps, 1)
                        pe.wait_ge(w_in[s], 32 * i + 32)
                        pe.wait_ge(xt_ready, item + 1)
                        for h in range(FH):
                            pe.wait_ge(rel_ready, item * FH + h + 1)
                            for o in range(KC):
                                last = pe.matmul(k.banks[1 + h][:, :], xt[:, o, :], key[s][:, o, h * 512:(h + 1) * 512], start=(o == 0), stop=(o == KC - 1))
                            last.then_inc(key_ps, 1)
                        for h in range(FH):
                            pe.wait_ge(sq_ready, item * FH + h + 1)
                            pe.wait_ge(hid_ready, item * FH + h + 1)
                            for f in range(KC):
                                last = pe.transpose(k.banks[3 + h][:, f * P:(f + 1) * P], sq[h][:, f * P:(f + 1) * P], k.ident[:])
                            last.then_inc(hid_ps, 1)
                        pe.wait_ge(yo_ready, item + 1)
                        for f in range(FC):
                            if f % KC == 0:
                                pe.wait_ge(hid_ready, item * FH + f // KC + 1 + FH)
                            last = pe.matmul(k.banks[5][:, :], hid[:, f, :], val[s][:, f, :], start=(f == 0), stop=(f == FC - 1))
                        last.then_inc(val_ps, 1)

            @block.scalar
            def _(act):
                pairs = pairs_of(act)
                act.sem_inc(rel_ready, FH)
                with act.Fori(0, pairs) as i:
                    for s in range(2):
                        item = 2 * i + s
                        for h in range(FH):
                            act.wait_ge(key_ps, item * FH + h + 1)
                            act.activation(rel[h][:], k.banks[1 + h][:, :], ACT.Relu).then_inc(rel_ready, 1)
                        act.wait_ge(yo_ready, item + 2)
                        act.dma_start(slots("expert_out", item), yo[s][:]).then_inc(y_out[s], 16)
                for s in range(2):
                    wait_alone(k, act, y_out[s], pairs * 16 + 16)

            @block.vector
            def _(dve):
                pairs = pairs_of(dve)
                dve.sem_inc(hid_ready, FH)
                dve.sem_inc(yo_ready, 1)
                for s in range(2):
                    dve.sem_inc(y_out[s], 16)
                with dve.Fori(0, pairs) as i:
                    for s in range(2):
                        item = 2 * i + s
                        dve.wait_ge(x_ps, item + 1)
                        dve.tensor_copy(xt[:].rearrange("p c t -> p (c t)"), k.banks[0][:, :]).then_inc(xt_ready, 1)
                        for h in range(FH):
                            dve.wait_ge(rel_ready, item * FH + h + 1 + FH)
                            dve.tensor_tensor(sq[h][:], rel[h][:], rel[h][:], ALU.mult).then_inc(sq_ready, 1)
                        for h in range(FH):
                            dve.wait_ge(hid_ps, item * FH + h + 1)
                            dve.tensor_copy(hid[:, h * KC:(h + 1) * KC].rearrange("p f t -> p (f t)"), k.banks[3 + h][:, :]).then_inc(hid_ready, 1)
                        dve.wait_ge(y_out[s], 16 * i + 16)
                        dve.wait_ge(val_ps, item + 1)
                        dve.tensor_copy(yo[s][:], k.banks[5][:, :]).then_inc(yo_ready, 1)
    clear_semaphores(nc, sems)


def combine(nc, k, dram, m, recept):
    tag = k.next_run()
    with ExitStack() as ctx:
        sb = lambda n, s, d=F32: ctx.enter_context(nc.sbuf_tensor(n + tag, s, d))
        sems = []

        def sem(n):
            sems.append(ctx.enter_context(nc.semaphore(n + tag)))
            return sems[-1]

        get = [[sb(f"get{i}_{n}", [P, 1], I32) for n in range(TPC)] for i in range(CM)]
        y = [sb(f"y_rows{i}", [P, TPC, D]) for i in range(CM)]
        ry = sb("r_times_y", [P, TPC, KC, P])
        idx_ready, yt_ps, mulled, added = (sem("y_" + n) for n in ("idx_ready", "yt_ps", "mulled", "added"))
        block = ctx.enter_context(nc.Block())

        @block.sync
        def _(sp):
            load_leaky(sp, k, dram)
            load_gru(sp, k, dram)

        @block.vector
        def _(dve):
            for i in range(CM):
                for n in range(TPC):
                    last = dve.tensor_copy(get[i][n][:], k.get[:, bass.ds((m * CM + i) * TH + (n // TH) * (NT // B) + n % TH, 1)])
                last.then_inc(idx_ready, 1)
            for i in range(CM):
                for n in range(TPC):
                    done = i * TPC + n + 1
                    b, h = n // TH, n % TH
                    dve.wait_ge(yt_ps, done)
                    if i > 0:
                        dve.wait_ge(added, done - TPC)
                    dve.tensor_tensor(ry[:, n], recept[:, i, :, h * P:(h + 1) * P, b],
                                      k.banks[i * TPC + n][:, :].rearrange("p (c t) -> p c t", c=KC), ALU.mult).then_inc(mulled, 1)
                    dve.wait_ge(mulled, done)
                    here = k.A[:, bass.ds(S + (m * CM + i) * (TC * S) + h * (P * S), P * S)].rearrange("p (t c b) -> p c t b", c=KC, b=B)[:, :, :, b]
                    dve.tensor_tensor(here, here, ry[:, n], ALU.add).then_inc(added, 1)

        @block.tensor
        def _(pe):
            for i in range(CM):
                for n in range(TPC):
                    pe.wait_ge(k.gathered[i][n], 16 * m + 16)
                    for o in range(KC):
                        last = pe.transpose(k.banks[i * TPC + n][:, o * P:(o + 1) * P], y[i][:, n, o * P:(o + 1) * P], k.ident[:])
                    last.then_inc(yt_ps, 1)

        @block.gpsimd
        def _(pool):
            for i in range(CM):
                pool.wait_ge(idx_ready, i + 1)
                for n in range(TPC):
                    pool.indirect_dma_start(out=y[i][:, n, :], out_offset=None, in_=dram["expert_out"][:, :],
                                            in_offset=bass.IndirectOffsetOnAxis(ap=get[i][n][:, 0:1], axis=0)).then_inc(k.gathered[i][n], 16)
    clear_semaphores(nc, sems)


def mixture(nc, k, dram, m):
    with nc.sbuf_tensor("recept" + k.next_run(), [P, CM, KC, TC, B], F32) as recept:
        experts(nc, k, dram, m, recept)
        combine(nc, k, dram, m, recept)


def adapted_layers(nc, k, dram):
    with ExitStack() as ctx:
        low = ctx.enter_context(nc.sbuf_tensor("low_rank", [RANK, 2, B, D], F32))
        base = ctx.enter_context(nc.sbuf_tensor("base", [P, KC, D], F32))
        low_in, base_in, low_ps, added = (ctx.enter_context(nc.semaphore("a_" + n)) for n in ("low_in", "base_in", "low_ps", "added"))
        block = ctx.enter_context(nc.Block())

        @block.sync
        def _(sp):
            for h in range(2):
                for b in range(B):
                    sp.dma_start(low[:, h, b, :], dram["xw"][b, h * RANK:(h + 1) * RANK, :]).then_inc(low_in, 16)
            sp.dma_start(base[:], dram["base"]).then_inc(base_in, 16)

        @block.tensor
        def _(pe):
            pe.wait_ge(low_in, 64)
            for b in range(B):
                for c in range(KC):
                    pe.matmul(k.banks[b * KC + c][:, :], low[:, 0, b, c * P:(c + 1) * P], low[:, 1, b, :], start=True, stop=True).then_inc(low_ps, 1)

        @block.vector
        def _(dve):
            dve.wait_ge(base_in, 16)
            for b in range(B):
                for c in range(KC):
                    dve.wait_ge(low_ps, b * KC + c + 1)
                    dve.tensor_tensor(k.layer[:, b, c, :], base[:, c, :], k.banks[b * KC + c][:, :], ALU.add).then_inc(added, 1)
    clear_semaphores(nc, [low_in, base_in, low_ps, added])


def adapted_output(nc, k, dram, out):
    with ExitStack() as ctx:
        sem = lambda n: ctx.enter_context(nc.semaphore(n))
        o_sb = [ctx.enter_context(nc.sbuf_tensor(f"out_sb{s}", [P, TC * S], F32)) for s in range(2)]
        out_ps, out_ready = sem("o_ps"), sem("o_ready")
        stored = [sem("o_stored0"), sem("o_stored1")]
        block = ctx.enter_context(nc.Block())

        @block.tensor
        def _(pe):
            with pe.Fori(0, CM) as c:
                for o in range(KC):
                    pe.wait_ge(out_ready, c * KC + o + 1)
                    for b in range(B):
                        for q in range(KC):
                            last = pe.matmul(k.banks[o][:, b * TC:(b + 1) * TC], k.layer[:, b, q, o * P:(o + 1) * P],
                                             chunk_steps(k.A, NCH - CM + c)[:, :, q, b], start=(q == 0 and b == 0), stop=(q == KC - 1),
                                             skip_group_check=True)
                    last.then_inc(out_ps, 1)

        @block.vector
        def _(dve):
            dve.sem_inc(out_ready, KC)
            dve.sem_inc(stored[0], 16)
            dve.sem_inc(stored[1], 16)
            with dve.Fori(0, CM // 2) as i:
                for s in range(2):
                    c = 2 * i + s
                    dve.wait_ge(stored[s], 16 * i + 16)
                    for o in range(KC):
                        dve.wait_ge(out_ps, c * KC + o + 1)
                        dve.scalar_tensor_tensor(o_sb[s][:].rearrange("p (t c b) -> p b t c", c=KC, b=B)[:, :, :, o],
                                                 chunk_steps(k.A, NCH - CM + c)[:, :, o, :].rearrange("p t b -> p b t"), 2.0,
                                                 k.banks[o][:, :].rearrange("p (b t) -> p b t", b=B), ALU.mult, ALU.add).then_inc(out_ready, 1)

        @block.sync
        def _(sp):
            with sp.Fori(0, CM // 2) as i:
                for s in range(2):
                    c = 2 * i + s
                    sp.wait_ge(out_ready, c * KC + 2 * KC)
                    sp.dma_start(out[:, bass.ds((NCH - CM + c) * (TC * S), TC * S)], o_sb[s][:]).then_inc(stored[s], 16)
            for s in range(2):
                sp.wait_ge(stored[s], 16 * (CM // 2) + 16)


class Kept:
    runs = 0

    def next_run(self):
        self.runs += 1
        return f"_run{self.runs}"


def cond_resid_program(nc, dram, out):
    dram["xw"] = nc.dram_tensor("adapter_rows", (B, NPIECE, D), F32, kind="Internal").ap()
    dram["expert_in"] = nc.dram_tensor("expert_in", (E * CAP + NTOK, D), F32, kind="Internal").ap()
    dram["expert_out"] = nc.dram_tensor("expert_out", (E * CAP + 1, D), F32, kind="Internal").ap()
    with ExitStack() as ctx:
        k = Kept()
        keep = lambda n, s, d=F32: ctx.enter_context(nc.sbuf_tensor(n, s, d))
        k.A = keep("acts", [P, (T + 1) * S])
        weights = keep("weights", [P, 2 * KC * F + 2 * FC * D])
        at = 0

        def part(pattern, **axes):
            nonlocal at
            size = 1
            for n in axes.values():
                size *= n
            at += size
            return weights[:, at - size:at].rearrange(pattern, **axes)

        k.wh = part("p (k n) -> p k n", k=KC, n=D)
        k.wz = part("p (k o n) -> p k o n", k=KC, o=KC, n=P)
        k.ug = part("p (g k n) -> p g k n", g=3, k=KC, n=D)
        k.wg = part("p (g k o n) -> p g k o n", g=3, k=KC, o=KC, n=P)
        at = 0
        k.key = [part("p (k n) -> p k n", k=KC, n=F) for _ in range(2)]
        k.val = [part("p (k n) -> p k n", k=FC, n=D) for _ in range(2)]
        k.vecs = keep("leaky_vectors", [P, 2, KC])
        k.leaky_in = ctx.enter_context(nc.semaphore("leaky_in"))
        k.gru_in = ctx.enter_context(nc.semaphore("gru_in"))
        k.hidden = keep("hidden", [P, S])
        k.vg = keep("gru_const", [P, 3, S])
        k.bgru = keep("gru_bias", [P, 3, KC])
        k.ident = keep("ident", [P, P])
        k.h_leaky = keep("h_leaky", [P, U * S])
        k.h_gru = keep("h_gru", [P, U * S])
        k.before = keep("before", [P, (NCH + 1) * S])
        k.put = keep("put", [P, NT], I32)
        k.get = keep("get", [P, NT], I32)
        k.pairs = keep("pairs", [1, NM], I32)
        k.banks = [ctx.enter_context(nc.psum_tensor(f"bank{n}", [P, 512], F32)) for n in range(8)]
        k.passed = ctx.enter_context(nc.semaphore("passed"))
        k.scattered = ctx.enter_context(nc.semaphore("scattered"))
        k.gathered = [[ctx.enter_context(nc.semaphore(f"gathered{i}_{n}")) for n in range(TPC)] for i in range(CM)]
        k.x_loaded = ctx.enter_context(nc.semaphore("x_loaded"))
        conditioning(nc, k, dram)
        routing(nc, k, dram)
        recurrences(nc, k, dram, 0, None)
        mixture(nc, k, dram, 0)
        with nc.Fori(1, NM) as m:
            recurrences(nc, k, dram, m, m - 1)
            mixture(nc, k, dram, m)
        k.layer = keep("layer", [P, B, KC, D])
        adapted_layers(nc, k, dram)
        recurrences(nc, k, dram, None, NM - 1, out)
        adapted_output(nc, k, dram, out)


def kernel(**inputs):
    import numpy as np
    import concourse.bacc as bacc
    from concourse.bass_utils import run_bass_kernel_spmd

    def features_first(a, *axes):
        a = np.ascontiguousarray(a)
        for ax in sorted((x % a.ndim for x in axes), reverse=True):
            s = a.shape
            a = a.reshape(s[:ax] + (4, 4, 32) + s[ax + 1:])
            a = np.moveaxis(a, ax + 1, ax)
            a = a.reshape(s[:ax] + (4, 128) + s[ax + 1:])
        return a

    def moving(w):
        return np.ascontiguousarray(features_first(w, 0).transpose(1, 0, 2))

    def stationary(w):
        return np.ascontiguousarray(features_first(w, 0, 1).transpose(1, 0, 2, 3))

    def vector(v):
        return features_first(v, 0).T

    a = {n: np.asarray(v) for n, v in inputs.items()}
    w0 = a["L0_cond_W"]
    x = features_first(a["x"], 2).transpose(3, 1, 2, 0)
    wk = features_first(a["L1_cond_w_key"], 1).transpose(0, 2, 1, 3)
    wv = features_first(a["L1_cond_w_value"], 2).reshape(E, FC, P, KC * P).transpose(0, 2, 1, 3)
    w2 = features_first(a["L3_cond_w2"], 0).reshape(KC, P, 2, KC, KC, 32, RANK)
    w2 = w2.transpose(1, 2, 6, 0, 4, 3, 5).reshape(P, NPIECE, KC, D)
    b2 = a["L3_cond_b2"].reshape(2, 4, 4, 32, RANK).transpose(0, 4, 2, 1, 3).reshape(1, NPIECE * D)
    arrays = {
        "x": x.reshape(P, T * S),
        "cond": features_first(a["cond_1024"], 1).transpose(2, 1, 0).reshape(P, S),
        "tok": a["itok_BxS_2_50255"].reshape(NT, P).T,
        "wh": moving(w0[:, :D].T),
        "wz": stationary(w0[:, D:].T),
        "l0v": np.stack([vector(a["L0_cond_b"]), vector(a["L0_cond_alpha"])], 1),
        "maa": np.stack([vector(a["L1_cond_time_maa_k"]), vector(a["L1_cond_time_maa_r"])], 1),
        "w_recept": stationary(a["L1_cond_w_recept"].T),
        "w_key": wk,
        "w_value": wv,
        "ug": np.stack([moving(a["L2_cond_" + n]) for n in ("U_z", "U_r", "U")]),
        "wg": np.stack([stationary(a["L2_cond_" + n]) for n in ("W_z", "W_r", "W")]),
        "cg": np.stack([stationary(a["L2_cond_" + n]) for n in ("C_z", "C_r", "C")]),
        "bgru": np.stack([vector(a["L2_cond_" + n]) for n in ("b_z", "b_r", "b")], 1),
        "base": stationary(a["L3_cond_base_layer"]).reshape(P, KC, D),
        "w1": stationary(a["L3_cond_w1"]),
        "w2": w2,
        "b2": np.broadcast_to(b2, (B, NPIECE * D)),
        "lnb": np.stack([vector(a["L3_cond_" + n]) for n in ("ln_g", "ln_b", "b1")], 1),
    }
    arrays = {f"in_{n}": np.ascontiguousarray(v) for n, v in arrays.items()}
    nc = bacc.Bacc("TRN2", target_bir_lowering=False, num_devices=1)
    dram = {n[3:]: nc.dram_tensor(n, v.shape, mybir.dt.from_np(v.dtype), kind="ExternalInput").ap() for n, v in arrays.items()}
    out = nc.dram_tensor("out", (P, T * S), F32, kind="ExternalOutput").ap()
    cond_resid_program(nc, dram, out)
    got = run_bass_kernel_spmd(nc, [arrays], core_ids=[0]).results[0]["out"]
    return np.ascontiguousarray(np.asarray(got).reshape(4, 32, T, KC, B).transpose(4, 2, 0, 3, 1).reshape(B, T, D))
```
